# Optimizing a Trainium2 kernel written in Bass

```python
import numpy as np
import jax
import jax.numpy as jnp

def _softmax(x, axis=-1):
    return jax.nn.softmax(x, axis=axis)

def _gelu(x):
    return jax.nn.gelu(x, approximate=True)

def _silu(x):
    return jax.nn.silu(x)

def _sigmoid(x):
    return jax.nn.sigmoid(x)

def _layernorm(x, axis=-1, eps=1e-05):
    m = jnp.mean(x, axis=axis, keepdims=True)
    v = jnp.var(x, axis=axis, keepdims=True)
    return (x - m) / jnp.sqrt(v + eps)

def _scatter_add(tgt, idx, src, axis=0):
    return tgt.at[idx].add(src)

def _segment_sum(src, seg, n):
    return jax.ops.segment_sum(src, seg, n)
kernel_name = 'mk_conv_attn_hybrid_d2_conv_nchw128_r4_519542'

def setup_inputs(seed: int=0):
    np.random.seed(seed)
    _w = jnp.asarray

    def _rec_inputs():
        import jax
        import jax.numpy as jnp
        _gk = jax.random.key(seed)
        x = -0.0002928 + 1 * jax.random.normal(jax.random.fold_in(_gk, 1), (8, 32, 16, 16), jnp.float32)
        return x
    x = _rec_inputs()

    def _L0_conv_setup():
        import jax, jax.numpy as jnp
        import numpy as np
        K = 3
        PAD = 1

        def conv2d(x, w, b, pad):
            out = jax.lax.conv_general_dilated(x, w, window_strides=(1, 1), padding=[(pad, pad), (pad, pad)], dimension_numbers=('NCHW', 'OIHW', 'NCHW'))
            return out + b[None, :, None, None]

        def bilinear_sample(x, ys, xs):
            B, C, H, W = x.shape
            y0f = jnp.floor(ys)
            x0f = jnp.floor(xs)
            iy0 = y0f.astype(jnp.int32)
            ix0 = x0f.astype(jnp.int32)
            iy1 = iy0 + 1
            ix1 = ix0 + 1
            wy1 = ys - y0f
            wy0 = 1.0 - wy1
            wx1 = xs - x0f
            wx0 = 1.0 - wx1
            b_idx = jnp.arange(B)[:, None, None, None]

            def fetch(iy, ix):
                valid = (iy >= 0) & (iy < H) & (ix >= 0) & (ix < W)
                iyc = jnp.clip(iy, 0, H - 1)
                ixc = jnp.clip(ix, 0, W - 1)
                v = x[b_idx, :, iyc, ixc]
                return v * valid[..., None].astype(x.dtype)
            return fetch(iy0, ix0) * (wy0 * wx0)[..., None] + fetch(iy0, ix1) * (wy0 * wx1)[..., None] + fetch(iy1, ix0) * (wy1 * wx0)[..., None] + fetch(iy1, ix1) * (wy1 * wx1)[..., None]
        key = jax.random.key(seed)
        k1, k2, k3, k4, k5 = jax.random.split(key, 5)
        B, C, H, W = (8, 32, 16, 16)
        O = 32
        K2 = K * K
        x = jax.random.normal(k1, (B, C, H, W), dtype=jnp.float32)
        offset_w = jax.random.normal(k2, (2 * K2, C, K, K), dtype=jnp.float32) * 0.01
        offset_b = jax.random.normal(k3, (2 * K2,), dtype=jnp.float32) * 0.01
        weight = jax.random.normal(k4, (O, C, K, K), dtype=jnp.float32) / np.sqrt(C * K2)
        bias = jax.random.normal(k5, (O,), dtype=jnp.float32) * 0.01
        return {'x': x, 'offset_w': offset_w, 'offset_b': offset_b, 'weight': weight, 'bias': bias}
    _L0_conv_all = _L0_conv_setup()
    _L0_conv_in = {k: v for k, v in _L0_conv_all.items() if k in ('offset_w', 'offset_b', 'weight', 'bias')}
    del _L0_conv_all

    def _L1_attn_setup():
        import jax, jax.numpy as jnp
        import numpy as np
        BATCH, LENGTH = (4, 128)
        D_MODEL, D_STATE, EXPAND = (32, 64, 2)
        D_INNER = EXPAND * D_MODEL
        key = jax.random.key(seed)
        ks = jax.random.split(key, 8)
        x = jax.random.normal(ks[0], (BATCH, LENGTH, D_MODEL), jnp.float32)
        W_in = jax.random.normal(ks[1], (D_MODEL, 2 * D_INNER), jnp.float32) / np.float32(np.sqrt(D_MODEL))
        W_delta = jax.random.normal(ks[2], (D_INNER, D_INNER), jnp.float32) * np.float32(0.005)
        W_B = jax.random.normal(ks[3], (D_INNER, D_STATE), jnp.float32) / np.float32(np.sqrt(D_INNER))
        W_C = jax.random.normal(ks[4], (D_INNER, D_INNER), jnp.float32) / np.float32(np.sqrt(D_INNER))
        W_out = jax.random.normal(ks[5], (D_INNER, D_MODEL), jnp.float32) / np.float32(np.sqrt(D_INNER))
        A = jax.random.normal(ks[6], (D_INNER, D_STATE), jnp.float32) * np.float32(0.02)
        D = jnp.ones((D_INNER,), jnp.float32)
        return dict(x=x, W_in=W_in, W_delta=W_delta, W_B=W_B, W_C=W_C, W_out=W_out, A=A, D=D)
    _L1_attn_all = _L1_attn_setup()
    _L1_attn_in = {k: v for k, v in _L1_attn_all.items() if k in ('W_in', 'W_delta', 'W_B', 'W_C', 'W_out', 'A', 'D')}
    del _L1_attn_all

    def _L1_ffn_setup():
        import jax, jax.numpy as jnp
        import numpy as np
        NB, NOPS = (33, 19)
        D, H = (32, 128)
        B, S = (8, 256)
        CARRY_OPS = [0, 1, 2, 10, 11, 12, 13]

        def _build_masks():
            am = np.zeros((NB, NOPS), dtype=bool)
            fm = np.zeros((NB, NOPS), dtype=bool)
            fm[0, :] = True
            for b in range(1, 8):
                am[b, CARRY_OPS] = True
                fm[b, CARRY_OPS] = True
            am[8, [14, 15, 8, 9]] = True
            fm[8, [14, 15, 8, 9]] = True
            for b in range(16, 32):
                fm[b, [3, 4]] = True
            am[32, [10, 11, 12, 13]] = True
            fm[32, [5, 6, 7, 2, 4, 10, 11, 12, 13]] = True
            return (jnp.asarray(am), jnp.asarray(fm))
        key = jax.random.key(seed)
        ks = jax.random.split(key, 9)
        sd = 1.0 / np.sqrt(D)
        sh = 1.0 / np.sqrt(H)
        am, fm = _build_masks()
        return {'x': jax.random.normal(ks[0], (B, S, D), jnp.float32), 'ffn_w1': jax.random.normal(ks[1], (NB, NOPS, D, H), jnp.float32) * sd, 'ffn_b1': jnp.zeros((NB, NOPS, H), jnp.float32), 'ffn_w2': jax.random.normal(ks[2], (NB, NOPS, H, D), jnp.float32) * sh, 'ffn_b2': jnp.zeros((NB, NOPS, D), jnp.float32), 'wq': jax.random.normal(ks[3], (NB, NOPS, D, D), jnp.float32) * sd, 'wk': jax.random.normal(ks[4], (NB, NOPS, D, D), jnp.float32) * sd, 'wv': jax.random.normal(ks[5], (NB, NOPS, D, D), jnp.float32) * sd, 'wo': jax.random.normal(ks[6], (NB, NOPS, D, D), jnp.float32) * sd, 'attn_mask': am, 'ffn_mask': fm}
    _L1_ffn_all = _L1_ffn_setup()
    _L1_ffn_in = {k: v for k, v in _L1_ffn_all.items() if k in ('ffn_w1', 'ffn_b1', 'ffn_w2', 'ffn_b2', 'wq', 'wk', 'wv', 'wo', 'attn_mask', 'ffn_mask')}
    del _L1_ffn_all
    return {'x': x, 'L0_conv_offset_w': _L0_conv_in['offset_w'], 'L0_conv_offset_b': _L0_conv_in['offset_b'], 'L0_conv_weight': _L0_conv_in['weight'], 'L0_conv_bias': _L0_conv_in['bias'], 'L1_attn_W_in': _L1_attn_in['W_in'], 'L1_attn_W_delta': _L1_attn_in['W_delta'], 'L1_attn_W_B': _L1_attn_in['W_B'], 'L1_attn_W_C': _L1_attn_in['W_C'], 'L1_attn_W_out': _L1_attn_in['W_out'], 'L1_attn_A': _L1_attn_in['A'], 'L1_attn_D': _L1_attn_in['D'], 'L1_ffn_ffn_w1': _L1_ffn_in['ffn_w1'], 'L1_ffn_ffn_b1': _L1_ffn_in['ffn_b1'], 'L1_ffn_ffn_w2': _L1_ffn_in['ffn_w2'], 'L1_ffn_ffn_b2': _L1_ffn_in['ffn_b2'], 'L1_ffn_wq': _L1_ffn_in['wq'], 'L1_ffn_wk': _L1_ffn_in['wk'], 'L1_ffn_wv': _L1_ffn_in['wv'], 'L1_ffn_wo': _L1_ffn_in['wo'], 'L1_ffn_attn_mask': _L1_ffn_in['attn_mask'], 'L1_ffn_ffn_mask': _L1_ffn_in['ffn_mask']}

def reference(x, L0_conv_offset_w, L0_conv_offset_b, L0_conv_weight, L0_conv_bias, L1_attn_W_in, L1_attn_W_delta, L1_attn_W_B, L1_attn_W_C, L1_attn_W_out, L1_attn_A, L1_attn_D, L1_ffn_ffn_w1, L1_ffn_ffn_b1, L1_ffn_ffn_w2, L1_ffn_ffn_b2, L1_ffn_wq, L1_ffn_wk, L1_ffn_wv, L1_ffn_wo, L1_ffn_attn_mask, L1_ffn_ffn_mask):
    import jax
    import jax.numpy as jnp

    def _L0_conv_ref(x, offset_w, offset_b, weight, bias):
        import jax, jax.numpy as jnp
        import numpy as np
        K = 3
        PAD = 1

        def conv2d(x, w, b, pad):
            out = jax.lax.conv_general_dilated(x, w, window_strides=(1, 1), padding=[(pad, pad), (pad, pad)], dimension_numbers=('NCHW', 'OIHW', 'NCHW'))
            return out + b[None, :, None, None]

        def bilinear_sample(x, ys, xs):
            B, C, H, W = x.shape
            y0f = jnp.floor(ys)
            x0f = jnp.floor(xs)
            iy0 = y0f.astype(jnp.int32)
            ix0 = x0f.astype(jnp.int32)
            iy1 = iy0 + 1
            ix1 = ix0 + 1
            wy1 = ys - y0f
            wy0 = 1.0 - wy1
            wx1 = xs - x0f
            wx0 = 1.0 - wx1
            b_idx = jnp.arange(B)[:, None, None, None]

            def fetch(iy, ix):
                valid = (iy >= 0) & (iy < H) & (ix >= 0) & (ix < W)
                iyc = jnp.clip(iy, 0, H - 1)
                ixc = jnp.clip(ix, 0, W - 1)
                v = x[b_idx, :, iyc, ixc]
                return v * valid[..., None].astype(x.dtype)
            return fetch(iy0, ix0) * (wy0 * wx0)[..., None] + fetch(iy0, ix1) * (wy0 * wx1)[..., None] + fetch(iy1, ix0) * (wy1 * wx0)[..., None] + fetch(iy1, ix1) * (wy1 * wx1)[..., None]
        B, C, H, W = x.shape
        K2 = K * K
        offsets = conv2d(x, offset_w, offset_b, PAD)
        off = offsets.reshape(B, K2, 2, H, W)
        dy = off[:, :, 0]
        dx = off[:, :, 1]
        kk = jnp.arange(K, dtype=jnp.float32)
        kh = jnp.repeat(kk, K)
        kw = jnp.tile(kk, K)
        ys = (jnp.arange(H, dtype=jnp.float32) - PAD)[None, None, :, None] + kh[None, :, None, None] + dy
        xs = (jnp.arange(W, dtype=jnp.float32) - PAD)[None, None, None, :] + kw[None, :, None, None] + dx
        sampled = bilinear_sample(x, ys, xs)
        w = weight.reshape(weight.shape[0], C, K2)
        out = jnp.einsum('bkhwc,ock->bohw', sampled, w)
        return out + bias[None, :, None, None]

    def _L1_attn_ref(x, W_in, W_delta, W_B, W_C, W_out, A, D):
        import jax, jax.numpy as jnp
        import numpy as np
        BATCH, LENGTH = (4, 128)
        D_MODEL, D_STATE, EXPAND = (32, 64, 2)
        D_INNER = EXPAND * D_MODEL
        x_proj = x @ W_in
        xs, z = jnp.split(x_proj, 2, axis=-1)
        delta = xs @ W_delta
        Bv = xs @ W_B
        Cv = xs @ W_C
        deltaA = jnp.exp(jnp.einsum('bld,dn->bldn', delta, A))
        deltaB = jnp.einsum('bld,bln->bldn', delta, Bv)

        def step(state, inp):
            dA_i, dB_i, x_i, C_i = inp
            state = dA_i * state + dB_i * x_i[:, None, :]
            y = jnp.einsum('bdn,bn->bd', state, C_i)
            return (state, y)
        init = jnp.zeros((x.shape[0], D_INNER, D_STATE), xs.dtype)
        inps = (jnp.moveaxis(deltaA, 1, 0), jnp.moveaxis(deltaB, 1, 0), jnp.moveaxis(xs, 1, 0), jnp.moveaxis(Cv, 1, 0))
        _, ys = jax.lax.scan(step, init, inps)
        y = jnp.moveaxis(ys, 0, 1)
        y = y * jax.nn.silu(z)
        return y @ W_out

    def _L1_ffn_ref(x, ffn_w1, ffn_b1, ffn_w2, ffn_b2, wq, wk, wv, wo, attn_mask, ffn_mask):
        import jax, jax.numpy as jnp
        import numpy as np
        NB, NOPS = (33, 19)
        D, H = (32, 128)
        B, S = (8, 256)
        CARRY_OPS = [0, 1, 2, 10, 11, 12, 13]

        def _build_masks():
            am = np.zeros((NB, NOPS), dtype=bool)
            fm = np.zeros((NB, NOPS), dtype=bool)
            fm[0, :] = True
            for b in range(1, 8):
                am[b, CARRY_OPS] = True
                fm[b, CARRY_OPS] = True
            am[8, [14, 15, 8, 9]] = True
            fm[8, [14, 15, 8, 9]] = True
            for b in range(16, 32):
                fm[b, [3, 4]] = True
            am[32, [10, 11, 12, 13]] = True
            fm[32, [5, 6, 7, 2, 4, 10, 11, 12, 13]] = True
            return (jnp.asarray(am), jnp.asarray(fm))
        scale = jnp.asarray(1.0 / np.sqrt(D), x.dtype)

        def step(h, p):
            op = jnp.argmax(h[0, 0, :NOPS])
            q = h @ p['wq'][op]
            k = h @ p['wk'][op]
            v = h @ p['wv'][op]
            attn = jax.nn.softmax(jnp.einsum('bqd,bkd->bqk', q, k) * scale, axis=-1)
            y = jnp.einsum('bqk,bkd->bqd', attn, v) @ p['wo'][op]
            h = jnp.where(p['am'][op], y, h)
            z = jax.nn.relu(h @ p['w1'][op] + p['b1'][op]) @ p['w2'][op] + p['b2'][op]
            h = jnp.where(p['fm'][op], z, h)
            return (h, None)
        xs = {'w1': ffn_w1, 'b1': ffn_b1, 'w2': ffn_w2, 'b2': ffn_b2, 'wq': wq, 'wk': wk, 'wv': wv, 'wo': wo, 'am': attn_mask, 'fm': ffn_mask}
        out, _ = jax.lax.scan(step, x, xs)
        return out

    def _gn(v, G=32, eps=1e-05):
        B_, C_, H_, W_ = v.shape
        g = v.reshape(B_, G, C_ // G, H_, W_)
        m = jnp.mean(g, axis=(2, 3, 4), keepdims=True)
        s = jnp.var(g, axis=(2, 3, 4), keepdims=True)
        return ((g - m) / jnp.sqrt(s + eps)).reshape(v.shape)

    def _ln_c(v, eps=1e-06):
        m = jnp.mean(v, axis=1, keepdims=True)
        s = jnp.var(v, axis=1, keepdims=True)
        return (v - m) / jnp.sqrt(s + eps)

    def _ln_t(v, eps=1e-05):
        m = jnp.mean(v, axis=-1, keepdims=True)
        s = jnp.var(v, axis=-1, keepdims=True)
        return (v - m) / jnp.sqrt(s + eps)

    def _to_tokens(v):
        B_, C_, H_, W_ = v.shape
        return v.reshape(B_, C_, H_ * W_).transpose(0, 2, 1)

    def _from_tokens(t, like):
        B_, C_, H_, W_ = like.shape
        return t.transpose(0, 2, 1).reshape(B_, C_, H_, W_)
    x = x + _L0_conv_ref(_gn(x), L0_conv_offset_w, L0_conv_offset_b, L0_conv_weight, L0_conv_bias)
    t = _to_tokens(x)
    t = t + _L1_attn_ref(_ln_t(t), L1_attn_W_in, L1_attn_W_delta, L1_attn_W_B, L1_attn_W_C, L1_attn_W_out, L1_attn_A, L1_attn_D)
    t = t + _L1_ffn_ref(_ln_t(t), L1_ffn_ffn_w1, L1_ffn_ffn_b1, L1_ffn_ffn_w2, L1_ffn_ffn_b2, L1_ffn_wq, L1_ffn_wk, L1_ffn_wv, L1_ffn_wo, L1_ffn_attn_mask, L1_ffn_ffn_mask)
    x = _from_tokens(t, x)
    return x

_drawn_inputs = setup_inputs


def setup_inputs(seed=0):
    import zlib

    import numpy as np

    out = dict(_drawn_inputs(seed))
    spreads = {'L1_attn_D': (1.0, 0.2), 'L1_ffn_ffn_b1': (0.0, 0.271), 'L1_ffn_ffn_b2': (0.0, 0.1)}
    factors = {'L1_attn_A': 7.792, 'L1_ffn_wq': 3.181, 'L1_ffn_wk': 3.364}
    for name, (base, spread) in spreads.items():
        noise = np.random.default_rng([zlib.crc32(name.encode()), seed]).standard_normal(out[name].shape)
        drawn = base * np.exp(spread * noise) if base else spread * noise
        out[name] = jnp.asarray(drawn.astype(out[name].dtype))
    for name, factor in factors.items():
        out[name] = (out[name] * factor).astype(out[name].dtype)
    return out
```

```python
from contextlib import ExitStack

import concourse.bass as bass
from concourse import mybir

B, C, HW = 8, 32, 256
SIDE = 16
PAIRS, HALVES = 4, 2
TAPS = 9
OFFS = 2 * TAPS
DI = 64
LAYERS, OPS, HID = 33, 19, 128
TOK = HALVES * HW
SEQ = PAIRS * HW
GN_EPS = 1e-5
BANK = 512
GROUPS, PER = 4, 16


def columns(sizes):
    at, out = 0, {}
    for name, size in sizes:
        out[name] = (at, at + size)
        at += size
    return out, at


CONST, CONST_W = columns([("offset_b", 1), ("conv_b", 1), ("eps", 1), ("pad", 1), ("level", SIDE), ("ident", 128),
                          ("average", 128), ("grid", TOK)])
SSM, SSM_W = columns([("w_in", 128), ("w_delta", 128), ("w_b", 128), ("w_c", 128), ("regroup", 128), ("w_out", C), ("a", DI)])


def hybrid_kernel(nc, x, const, offset_w, conv_w, ssm_w, spread_w, masks, steps, w_attn, w_up, w_down, out):
    f32, bf16, i32, u32, u8 = (mybir.dt.float32, mybir.dt.bfloat16, mybir.dt.int32, mybir.dt.uint32, mybir.dt.uint8)
    ALU = mybir.AluOpType
    ACT = mybir.ActivationFunctionType
    AX = mybir.AxisListType
    SCALE = 1.0 / C ** 0.5

    ctx = ExitStack()
    with ctx:
        def sb(name, shape, dt=f32):
            return ctx.enter_context(nc.sbuf_tensor(name, shape, dt))

        def sem(name):
            return ctx.enter_context(nc.semaphore(name))

        cst = sb("cst", [128, CONST_W])
        offw = sb("offw", [128, TAPS * 128])
        convw = sb("convw", [128, TAPS * C])
        ssmw = sb("ssmw", [128, SSM_W])
        spread = sb("spread", [96, 32], bf16)
        picks = sb("picks", [96, PER * 128], bf16)
        zero_bf = sb("zero_bf", [128, BANK], bf16)
        part = {n: cst[:, a:b] for n, (a, b) in CONST.items()}
        wt = {n: ssmw[:, a:b] for n, (a, b) in SSM.items()}
        ident = part["ident"]

        xq = sb("xq", [128, TOK])
        t1 = sb("t1", [128, TOK])
        t2 = sb("t2", [128, TOK])
        cen = sb("cen", [128, TOK])
        sq = sb("sq", [128, TOK])
        sd = sb("sd", [128, TOK])
        rs = sb("rs", [128, TOK])
        tn = sb("tn", [128, TOK])
        h = sb("h", [128, TOK])
        fin = sb("fin", [128, TOK])
        stats = sb("stats", [128, HALVES, 6])
        mv = sb("mv", [128, HALVES, 2])
        gsd = sb("gsd", [128, HALVES])
        grs = sb("grs", [128, HALVES])

        pool = sb("pool", [128, 30 * 1024])
        used = {"conv": 0, "ssm": 0, "ffn": 0}

        def region(phase, n):
            a = used[phase]
            used[phase] = a + n
            assert used[phase] <= 30 * 1024
            return pool[:, a:a + n]

        PADDED = SIDE + 2
        xpad = region("conv", HALVES * PADDED * PADDED).rearrange("p (b y x) -> p b y x", b=HALVES, y=PADDED)
        xn = region("conv", TOK)
        off = region("conv", TOK)
        hat = region("conv", 16 * OFFS * SIDE).rearrange("p (c o y) -> p c o y", c=16, o=OFFS)
        zs = region("conv", 16 * TAPS * C).rearrange("p (b q h k) -> p b q h k", b=HALVES, q=PAIRS, h=2)
        samp = [region("conv", 8 * HW).rearrange("p (c n) -> p c n", c=8) for _ in range(3)]
        sampT = [region("conv", 8 * HW).rearrange("p (q h n) -> p q h n", q=PAIRS, h=2) for _ in range(3)]
        zk = [region("conv", 8 * C).rearrange("p (q h o) -> p q h o", q=PAIRS, h=2) for _ in range(3)]

        xs = region("ssm", SEQ)
        ez = region("ssm", SEQ)
        sz = region("ssm", SEQ)
        delta = region("ssm", SEQ)
        bx = region("ssm", SEQ)
        xg = region("ssm", SEQ)
        rest = [region("ssm", SEQ) for _ in range(2)]
        pieces = [[region("ssm", SEQ // 2).bitcast(bf16) for _ in range(3)] for _ in range(2)]
        stack = [region("ssm", GROUPS * SEQ // 2).bitcast(bf16) for _ in range(2)]
        dA = [region("ssm", SEQ) for _ in range(2)]
        dBx = [region("ssm", SEQ) for _ in range(2)]
        state = [region("ssm", SEQ) for _ in range(2)]
        cs = [region("ssm", SEQ) for _ in range(2)]
        prod = [region("ssm", SEQ) for _ in range(2)]
        gated = region("ssm", SEQ)

        wat = region("ffn", 128)
        wbd = region("ffn", 4 * 128).rearrange("p (w n) -> p w n", w=4)
        wup = region("ffn", HID + 1)
        region("ffn", 3)
        wdn = region("ffn", C + 1)
        region("ffn", 3)
        qs, ks, vs, on, ot = (region("ffn", TOK) for _ in range(5))
        es = [region("ffn", 1024).rearrange("p (c k) -> p c k", c=4) for _ in range(2)]
        pt = [region("ffn", 1024) for _ in range(2)]
        mx = region("ffn", 16)
        nm = region("ffn", 16)
        sm = region("ffn", 16)
        ri = region("ffn", 16)
        hid = region("ffn", PAIRS * TOK).rearrange("p (q n) -> p q n", q=PAIRS)
        row = sb("row", [1, 32])
        top = sb("top", [1, 8])
        idx = sb("idx", [1, 8], u32)
        mask8 = sb("mask8", [1, 2 * OPS * LAYERS], u8)
        stepno = sb("stepno", [1, 2 * LAYERS])
        tab = sb("tab", [1, OPS * 3 * LAYERS])
        cand = sb("cand", [1, 3 * LAYERS])
        best = sb("best", [1, 4])
        cur = sb("cur", [1, 1])
        ctl = sb("ctl", [1, 4], i32)

        ps = ctx.enter_context(nc.psum_tensor("ps", [128, 8 * BANK], f32))

        def bank(i, n=1):
            return ps[:, i * BANK:(i + n) * BANK]

        x_in, const_in, offw_in, convw_in, ssmw_in, spread_in, ctl_in = map(
            sem, ["x_in", "const_in", "offw_in", "convw_in", "ssmw_in", "spread_in", "ctl_in"])
        picks_ready, hat_abs = sem("picks_ready"), sem("hat_abs")
        pad_zeroed, zero_set, wbd_zeroed = map(sem, ["pad_zeroed", "zero_set", "wbd_zeroed"])
        dve_step, act_step, pool_step = map(sem, ["dve_step", "act_step", "pool_step"])
        gn_var, gn_sd, xn_ready = map(sem, ["gn_var", "gn_sd", "xn_ready"])
        off_done, off_ready, offT_done, hat_diff, hat_ready = map(
            sem, ["off_done", "off_ready", "offT_done", "hat_diff", "hat_ready"])
        z_done, z_ready = map(sem, ["z_done", "z_ready"])
        samp_made = [sem(f"samp_made{j}") for j in range(3)]
        samp_turned, turned_ready, zk_ready, chunk_summed, conv_done = map(
            sem, ["samp_turned", "turned_ready", "zk_ready", "chunk_summed", "conv_done"])
        ln_in, ln_mean, ln_cen, ln_sq, ln_var, ln_sd, ln_out = map(
            sem, ["ln_in", "ln_mean", "ln_cen", "ln_sq", "ln_var", "ln_sd", "ln_out"])
        xz_done, xs_ready, ez_ready, dbc_done, delta_ready, gate_ready = map(
            sem, ["xz_done", "xs_ready", "ez_ready", "dbc_done", "delta_ready", "gate_ready"])
        xg_ready, bx_ready = sem("xg_ready"), sem("bx_ready")
        part_cast, part_rest, stack_in = [sem("b_cast"), sem("c_cast")], [sem("b_rest"), sem("c_rest")], sem("stack_in")
        b_spread, c_spread, c_ready, da_ready, dbx_ready, scanned, prod_ready, prod_summed, y_done = map(
            sem, ["b_spread", "c_spread", "c_ready", "da_ready", "dbx_ready", "scanned", "prod_ready", "prod_summed",
                  "y_done"])
        gated_ready, mix_done, da_zeroed = map(sem, ["gated_ready", "mix_done", "da_zeroed"])
        h_ready, row_done, ctl_step, ctl_words, ctl_ready, ctl_read, held, w_in = map(
            sem, ["h_ready", "row_done", "ctl_step", "ctl_words", "ctl_ready", "ctl_read", "held", "w_in"])
        bd_ready, qkv_done, qv_ready, k_ready, score_done, max_ready, exp_done, probT_done, probT_ready = map(
            sem, ["bd_ready", "qkv_done", "qv_ready", "k_ready", "score_done", "max_ready", "exp_done", "probT_done",
                  "probT_ready"])
        pv_done, head_ready, headT_done, headT_ready, attn_out, attn_step = map(
            sem, ["pv_done", "head_ready", "headT_done", "headT_ready", "attn_out", "attn_step"])
        up_done, act_relu, dve_relu, down_done = map(sem, ["up_done", "act_relu", "dve_relu", "down_done"])
        fin_ready, out_stored = map(sem, ["fin_ready", "out_stored"])

        block = ctx.enter_context(nc.Block())

        CHUNK_IT = 3

        def hold(eng, semaphore, value):
            eng.wait_ge(semaphore, value)
            eng.sem_inc(held, 1)

        def load_control(eng, regs):
            eng.load(regs, ctl[0:1, 0:4])
            eng.sem_inc(ctl_read, 1)

        def control_registers(eng, tag):
            return [eng.alloc_register(f"{tag}_{n}") for n in ("layer", "op", "attn", "ffn")]

        def counters(eng, tag):
            regs = [eng.alloc_register(f"{tag}_{n}") for n in ("steps", "attns", "ffns")]
            for r in regs:
                eng.reg_mov(r, 0)
            return regs

        @block.sync
        def _(sp):
            for half in range(HALVES):
                sp.dma_start(xq[:, half * HW:(half + 1) * HW], x[half]).then_inc(x_in, 16)
            sp.dma_start(cst[:, :], const).then_inc(const_in, 16)
            sp.dma_start(convw[:, :], conv_w).then_inc(convw_in, 16)
            sp.dma_start(ssmw[:, :], ssm_w).then_inc(ssmw_in, 16)
            sp.dma_start(spread[:, :], spread_w).then_inc(spread_in, 16)
            sp.dma_start(mask8[:, :], masks).then_inc(ctl_in, 16)
            sp.dma_start(stepno[:, :], steps).then_inc(ctl_in, 16)

            for t in range(2):
                for p in range(3):
                    sp.wait_ge(part_cast[t], p + 1)
                    for g in range(GROUPS):
                        sp.dma_start(stack[t][32 * p:32 * p + 32, g * SEQ:(g + 1) * SEQ],
                                     pieces[t][p][32 * g:32 * g + 32, :]).then_inc(stack_in, 16)

            regs = control_registers(sp, "sp")
            steps_done, _, _ = counters(sp, "sp")
            layer, op = regs[0], regs[1]
            sp.wait_ge(ctl_ready, 1)
            load_control(sp, regs)
            with sp.While(lambda: sp.snap(layer) < LAYERS):
                sp.reg_add(steps_done, steps_done, 1)
                at = sp.snap(sp.snap(layer) * OPS + sp.snap(op), min_val=0, max_val=LAYERS * OPS - 1)
                sp.dma_start(wup, w_up[bass.ds(at, 1), :, :].rearrange("o c n -> (o c) n").unsqueeze(0)
                             .broadcast_to([PAIRS, C, HID + 1])).then_inc(w_in, 16)
                sp.dma_start(wdn, w_down[bass.ds(at, 1), :, :].rearrange("o c n -> (o c) n")).then_inc(w_in, 16)
                sp.dma_start(wat, w_attn[bass.ds(at, 1), :, :].rearrange("o c n -> (o c) n").unsqueeze(0)
                             .broadcast_to([PAIRS, C, 128])).then_inc(w_in, 16)
                hold(sp, ctl_ready, sp.snap(steps_done) + 1)
                load_control(sp, regs)

            sp.wait_ge(fin_ready, 1)
            for half in range(HALVES):
                sp.dma_start(out[half], fin[:, half * HW:(half + 1) * HW]).then_inc(out_stored, 16)
            sp.wait_ge(out_stored, 16 * HALVES)

        @block.gpsimd
        def _(pool_e):
            pool_e.memset(xpad, 0.0).then_inc(pad_zeroed, 1)
            pool_e.memset(zero_bf[:, :], 0.0).then_inc(zero_set, 1)
            pool_e.sem_inc(chunk_summed, 3)
            pool_e.wait_ge(spread_in, 16)
            pool_e.tensor_copy(picks[:, :].rearrange("p (j b d) -> p b j d", j=PER, b=HALVES),
                               spread[:, :].rearrange("p (b j) -> p b j", b=HALVES).unsqueeze(3)
                               .broadcast_to([96, HALVES, PER, DI])).then_inc(picks_ready, 1)

            def sampling_chunk(it, half, kk, j):
                pool_e.wait_ge(samp_turned, 6 * it + 2 * j + 2)
                k = 3 * kk + j
                hy = hat[:, 8 * half:8 * half + 8, bass.ds(2 * k, 1), :].rearrange("p c o y -> p c (o y)")
                hx = hat[:, 8 * half:8 * half + 8, bass.ds(2 * k + 1, 1), :].rearrange("p c o y -> p c (o y)")
                pool_e.tensor_tensor(samp[j].rearrange("p c (y x) -> p c y x", y=SIDE),
                                     hy.unsqueeze(3).broadcast_to([128, 8, SIDE, SIDE]),
                                     hx.unsqueeze(2).broadcast_to([128, 8, SIDE, SIDE]),
                                     ALU.mult).then_inc(samp_made[j], 1)

            for half in range(HALVES):
                pool_e.wait_ge(z_ready, 2 * HALVES)
                pool_e.wait_ge(hat_ready, half + 1)
                with pool_e.Fori(0, CHUNK_IT) as kk:
                    it = kk + CHUNK_IT * half
                    for j in range(3):
                        k = 3 * kk + j
                        pool_e.wait_ge(chunk_summed, 3 * it + j + 1)
                        pool_e.tensor_copy(zk[j], zs[:, half, :, :, bass.ds(k * C, C)]).then_inc(zk_ready, 1)
                        if j == 2:
                            sampling_chunk(it, half, kk, j)

            pool_e.wait_ge(conv_done, 1)
            for t in range(2):
                pool_e.memset(prod[t], 0.0).then_inc(pool_step, 1)
            for t in range(2):
                pool_e.memset(dA[t], 0.0).then_inc(da_zeroed, 1)
            pool_e.wait_ge(pool_step, 2)
            pool_e.sem_inc(prod_ready, 2)
            with pool_e.Fori(0, DI // 2) as it:
                for r in range(2):
                    n = 2 * it + r
                    pool_e.wait_ge(scanned, n + 3)
                    pool_e.wait_ge(c_ready, n + 2)
                    pool_e.wait_ge(prod_summed, n + 1)
                    pool_e.tensor_tensor(prod[r], state[r], cs[r], ALU.mult).then_inc(prod_ready, 1)

        @block.scalar
        def _(act):
            act.dma_start(offw[:, :], offset_w).then_inc(offw_in, 16)
            act.wait_ge(const_in, 16)
            act.wait_ge(gn_var, 2)
            act.activation(gsd[:, :], mv[:, :, 1], ACT.Sqrt, bias=part["eps"]).then_inc(gn_sd, 1)

            act.sem_inc(turned_ready, 3)

            def evacuate_filters(n):
                act.wait_ge(z_done, n + 1)
                half, side = divmod(n, 2)
                act.activation(zs[:, half, :, side, :], bank(3, 4).rearrange("p (q k) -> p q k", q=PAIRS)
                               [:, :, 0:TAPS * C], ACT.Copy).then_inc(z_ready, 1)

            def hats(half):
                act.wait_ge(hat_diff, half + 1)
                v = hat[:, 8 * half:8 * half + 8, :, :].rearrange("p c o y -> p (c o y)")
                act.activation(v, v, ACT.Abs).then_inc(hat_abs, 1)
                act.wait_ge(hat_abs, half + 1)
                act.activation(v, v, ACT.Relu, bias=1.0, scale=-1.0).then_inc(hat_ready, 1)

            evacuate_filters(0)
            evacuate_filters(1)
            hats(0)
            evacuate_filters(2)
            evacuate_filters(3)
            hats(1)

            for half in range(HALVES):
                with act.Fori(0, CHUNK_IT) as kk:
                    it = kk + CHUNK_IT * half
                    for j in range(3):
                        act.wait_ge(chunk_summed, 3 * it + j + 1)
                        for side in range(2):
                            s = 2 * j + side
                            act.wait_ge(samp_turned, 6 * it + s + 7)
                            act.activation(sampT[j][:, 2 * side:2 * side + 2].rearrange("p q h n -> p (q h n)"),
                                           bank(2 + 2 * (s % 3), 2), ACT.Copy).then_inc(turned_ready, 1)

            def layer_norm(n):
                act.wait_ge(ln_cen, n + 1)
                act.activation(sq[:, :], cen[:, :], ACT.Square).then_inc(ln_sq, 1)
                act.wait_ge(ln_var, n + 1)
                act.activation(sd[:, :], bank(1), ACT.Sqrt, bias=part["eps"]).then_inc(ln_sd, 1)

            layer_norm(0)
            xz = bank(0, 4).rearrange("p (q s n) -> p q s n", q=PAIRS, s=2)
            act.wait_ge(xz_done, 1)
            act.activation(xs.rearrange("p (q n) -> p q n", q=PAIRS), xz[:, :, 0, :], ACT.Copy).then_inc(xs_ready, 1)
            act.activation(ez.rearrange("p (q n) -> p q n", q=PAIRS), xz[:, :, 1, :], ACT.Exp, scale=-1.0)\
               .then_inc(ez_ready, 1)
            act.wait_ge(dbc_done, 3)
            act.activation(xg, bank(2, 2), ACT.Copy).then_inc(xg_ready, 1)
            for t in range(2):
                if t:
                    act.wait_ge(dbc_done, 4)
                else:
                    act.wait_ge(bx_ready, 1)
                act.activation(pieces[t][0], bank(0, 2) if t else bx, ACT.Copy).then_inc(part_cast[t], 1)
                act.wait_ge(part_rest[t], 1)
                act.activation(pieces[t][1], rest[t], ACT.Copy).then_inc(part_cast[t], 1)

            act.wait_ge(delta_ready, 1)
            act.wait_ge(da_zeroed, 2)
            act.sem_inc(c_ready, 1)

            def inner_tail(ap):
                return ap.rearrange("p (q n) -> p q n", q=PAIRS)[:, :, 1:HW]

            with act.Fori(0, DI // 2) as it:
                for r in range(2):
                    n = 2 * it + r
                    act.wait_ge(scanned, n + 1)
                    act.activation(inner_tail(dA[r]), inner_tail(delta), ACT.Exp,
                                   scale=wt["a"][:, bass.ds(n, 1)]).then_inc(da_ready, 1)
                    act.wait_ge(c_spread, n + 1)
                    act.wait_ge(prod_ready, n + 1)
                    act.activation(cs[r], bank(6, 2), ACT.Copy).then_inc(c_ready, 1)

            layer_norm(1)

            regs = control_registers(act, "act")
            steps_done, attns, ffns = counters(act, "act")
            act.wait_ge(ctl_ready, 1)
            load_control(act, regs)
            with act.While(lambda: act.snap(regs[0]) < LAYERS):
                act.reg_add(steps_done, steps_done, 1)
                with act.If(act.snap(regs[2]) > 0):
                    a = act.snap(attns)
                    act.wait_ge(qkv_done, 3 * a + 1)
                    act.activation(qs, bank(0), ACT.Copy).then_inc(qv_ready, 1)
                    act.wait_ge(qkv_done, 3 * a + 3)
                    act.activation(vs, bank(2), ACT.Copy).then_inc(qv_ready, 1)
                    for q in range(PAIRS):
                        act.wait_ge(max_ready, PAIRS * a + q + 1)
                        if q >= 2:
                            act.wait_ge(probT_done, PAIRS * a + q - 1)
                        for c in range(4):
                            i = 4 * q + c
                            act.activation(es[q % 2][:, c, :], bank(4 + 2 * (q % 2), 2)[:, c * HW:(c + 1) * HW],
                                           ACT.Exp, bias=nm[:, i:i + 1], scale=SCALE,
                                           accum_out=sm[:, i:i + 1]).then_inc(exp_done, 1)
                    act.reg_add(attns, attns, 1)
                with act.If(act.snap(regs[3]) > 0):
                    f = act.snap(ffns)
                    act.wait_ge(w_in, act.snap(steps_done) * 48)
                    for q in range(2):
                        act.wait_ge(up_done, PAIRS * f + q + 1)
                        act.activation(hid[:, q, :], bank(4 + q), ACT.Relu, bias=wdn[:, C:C + 1]).then_inc(act_relu, 1)
                    act.reg_add(ffns, ffns, 1)
                hold(act, ctl_ready, act.snap(steps_done) + 1)
                load_control(act, regs)

        @block.vector
        def _(dve):
            made = [0]

            def step(ins):
                ins.then_inc(dve_step, 1)
                made[0] += 1

            def settle():
                dve.wait_ge(dve_step, made[0])

            dve.wait_ge(x_in, 16 * HALVES)
            for half in range(HALVES):
                step(dve.bn_stats(stats[:, half, :], xq[:, half * HW:(half + 1) * HW]))
            settle()
            for half in range(HALVES):
                dve.bn_aggr(mv[:, half, :], stats[:, half, :]).then_inc(gn_var, 1)
            dve.wait_ge(gn_sd, 1)
            step(dve.reciprocal(grs[:, :], gsd[:, :]))
            settle()
            dve.wait_ge(gn_var, 2)
            dve.wait_ge(pad_zeroed, 1)
            for half in range(HALVES):
                dve.tensor_scalar(xpad[:, half, 1:1 + SIDE, 1:1 + SIDE],
                                  xq[:, half * HW:(half + 1) * HW].rearrange("p (y x) -> p y x", y=SIDE),
                                  mv[:, half, 0:1], grs[:, half:half + 1], ALU.subtract, ALU.mult)\
                   .then_inc(xn_ready, 1)
            dve.wait_ge(xn_ready, HALVES)
            dve.tensor_copy(xn.rearrange("p (b y x) -> p b y x", b=HALVES, y=SIDE),
                            xpad[:, :, 1:1 + SIDE, 1:1 + SIDE]).then_inc(xn_ready, 1)

            dve.wait_ge(off_done, 1)
            dve.wait_ge(const_in, 16)
            dve.scalar_tensor_tensor(off, bank(2), part["offset_b"], part["grid"], ALU.add, ALU.add)\
               .then_inc(off_ready, 1)
            dve.wait_ge(offT_done, 1)
            for half in range(HALVES):
                pos = bank(1)[:, half * HW:(half + 1) * HW].rearrange("p (c o) -> p c o", c=8)[:, :, 0:OFFS]
                v = hat[:, 8 * half:8 * half + 8, :, :]
                dve.tensor_tensor(v, pos.unsqueeze(3).broadcast_to([128, 8, OFFS, SIDE]),
                                  part["level"].unsqueeze(1).unsqueeze(1).broadcast_to([128, 8, OFFS, SIDE]),
                                  ALU.subtract).then_inc(hat_diff, 1)

            for half in range(HALVES):
                dve.wait_ge(hat_ready, half + 1)
                with dve.Fori(0, CHUNK_IT) as kk:
                    it = kk + CHUNK_IT * half
                    for j in range(2):
                        k = 3 * kk + j
                        dve.wait_ge(samp_turned, 6 * it + 2 * j + 2)
                        hy = hat[:, 8 * half:8 * half + 8, bass.ds(2 * k, 1), :].rearrange("p c o y -> p c (o y)")
                        hx = hat[:, 8 * half:8 * half + 8, bass.ds(2 * k + 1, 1), :].rearrange("p c o y -> p c (o y)")
                        dve.tensor_tensor(samp[j].rearrange("p c (y x) -> p c y x", y=SIDE),
                                          hy.unsqueeze(3).broadcast_to([128, 8, SIDE, SIDE]),
                                          hx.unsqueeze(2).broadcast_to([128, 8, SIDE, SIDE]),
                                          ALU.mult).then_inc(samp_made[j], 1)

            dve.wait_ge(conv_done, 1)
            dve.tensor_scalar(t1[:, :], bank(0), part["conv_b"], None, ALU.add).then_inc(ln_in, 1)

            def layer_norm(n, src, dst):
                dve.wait_ge(ln_in, n + 1)
                dve.wait_ge(ln_mean, n + 1)
                dve.tensor_tensor(cen[:, :], src[:, :], bank(1), ALU.subtract).then_inc(ln_cen, 1)
                dve.wait_ge(ln_sd, n + 1)
                step(dve.reciprocal(rs[:, :], sd[:, :]))
                settle()
                dve.wait_ge(ln_cen, n + 1)
                return dve.tensor_tensor(dst[:, :], cen[:, :], rs[:, :], ALU.mult)

            layer_norm(0, t1, tn).then_inc(ln_out, 1)

            dve.wait_ge(ctl_in, 32)
            tabv = tab[:, :].rearrange("p (o s l) -> p o s l", o=OPS, s=3)
            m8 = mask8[:, :].rearrange("p (s o l) -> p s o l", s=2, o=OPS)
            left = stepno[:, LAYERS:2 * LAYERS].unsqueeze(1).broadcast_to([1, OPS, LAYERS])
            for s in range(2):
                step(dve.tensor_tensor(tabv[:, :, 1 + s, :], m8[:, s, :, :], left, ALU.mult))
            settle()
            step(dve.tensor_tensor(tabv[:, :, 0, :], tabv[:, :, 1, :], tabv[:, :, 2, :], ALU.max))
            step(dve.memset(cur[:, :], -1.0))

            def inner(ap):
                return ap.rearrange("p (q n) -> p q n", q=PAIRS)

            dve.wait_ge(xs_ready, 1)
            dve.wait_ge(ez_ready, 1)
            dve.wait_ge(dbc_done, 1)
            dve.tensor_copy(delta, bank(4, 2)).then_inc(delta_ready, 1)
            step(dve.tensor_scalar(ez, ez, 1.0, None, ALU.add))
            settle()
            step(dve.reciprocal(ez, ez))
            settle()
            xz = bank(0, 4).rearrange("p (q s n) -> p q s n", q=PAIRS, s=2)
            dve.tensor_tensor(inner(sz), inner(ez), xz[:, :, 1, :], ALU.mult).then_inc(gate_ready, 1)
            dve.wait_ge(dbc_done, 2)
            dve.wait_ge(xg_ready, 1)
            dve.tensor_tensor(bx, xg, bank(6, 2), ALU.mult).then_inc(bx_ready, 1)
            dve.wait_ge(bx_ready, 1)
            for t in range(2):
                dve.wait_ge(part_cast[t], 1)
                dve.tensor_tensor(rest[t], bank(0, 2) if t else bx, pieces[t][0], ALU.subtract).then_inc(part_rest[t], 1)
                dve.wait_ge(part_cast[t], 2)
                dve.tensor_tensor(pieces[t][2], rest[t], pieces[t][1], ALU.subtract).then_inc(part_cast[t], 1)

            dve.wait_ge(delta_ready, 1)
            dve.sem_inc(dbx_ready, 2)
            dve.sem_inc(scanned, 2)
            with dve.Fori(0, DI // 2) as it:
                for r in range(2):
                    n = 2 * it + r
                    dve.wait_ge(b_spread, n + 1)
                    dve.wait_ge(scanned, n + 1)
                    dve.tensor_tensor(dBx[r], delta, bank(2 + 2 * r, 2), ALU.mult).then_inc(dbx_ready, 1)
                    dve.wait_ge(dbx_ready, n + 3)
                    dve.wait_ge(da_ready, n + 1)
                    dve.wait_ge(prod_ready, n + 1)
                    dve.tensor_tensor_scan(state[r], dA[r], dBx[r], 0.0, ALU.mult, ALU.add).then_inc(scanned, 1)

            dve.wait_ge(y_done, 1)
            dve.wait_ge(gate_ready, 1)
            dve.tensor_tensor(gated, bank(0, 2), sz, ALU.mult).then_inc(gated_ready, 1)
            dve.wait_ge(mix_done, 1)
            for half in range(HALVES):
                ins = dve.tensor_tensor(t2[:, half * HW:(half + 1) * HW], t1[:, half * HW:(half + 1) * HW],
                                        bank(2 + half)[:, 0:HW], ALU.add)
                if half:
                    ins.then_inc(ln_in, 1)
                else:
                    step(ins)
            settle()
            layer_norm(1, t2, h).then_inc(h_ready, 1)
            step(dve.memset(wbd, 0.0))
            settle()

            regs = control_registers(dve, "dve")
            steps_done, attns, ffns = counters(dve, "dve")
            op_reg = dve.alloc_register("dve_chosen")

            def next_step(n):
                dve.wait_ge(row_done, n + 1)
                c = 7 * n
                dve.tensor_copy(row[:, :], bank(3)[0:1, 0:32]).then_inc(ctl_step, 1)
                hold(dve, ctl_step, c + 1)
                dve.max(top[:, :], row[:, 0:OPS]).then_inc(ctl_step, 1)
                hold(dve, ctl_step, c + 2)
                dve.max_index(idx[:, :], top[:, :], row[:, 0:OPS]).then_inc(ctl_step, 1)
                hold(dve, ctl_step, c + 3)
                dve.load([op_reg], idx[0:1, 0:1])
                op = dve.snap(op_reg, min_val=0, max_val=OPS - 1)
                v = cand[:, :].rearrange("p (s l) -> p s l", s=3)
                dve.scalar_tensor_tensor(v, stepno[:, 0:LAYERS].unsqueeze(1).broadcast_to([1, 3, LAYERS]), cur[:, 0:1],
                                         tab[:, bass.ds(op * (3 * LAYERS), 3 * LAYERS)]
                                         .rearrange("p (s l) -> p s l", s=3), ALU.is_gt, ALU.mult).then_inc(ctl_step, 1)
                dve.wait_ge(ctl_step, c + 4)
                dve.tensor_reduce(best[:, 0:3], v, AX.X, ALU.max).then_inc(ctl_step, 1)
                dve.wait_ge(ctl_step, c + 5)
                dve.tensor_scalar(cur[:, :], best[:, 0:1], -1.0, float(LAYERS), ALU.mult, ALU.add).then_inc(ctl_step, 1)
                dve.wait_ge(ctl_read, 3 * n + 1)
                dve.tensor_scalar(ctl[:, 2:4], best[:, 1:3], best[:, 0:1], None, ALU.is_equal).then_inc(ctl_step, 1)

            def publish(n):
                dve.tensor_copy(ctl[:, 1:2], idx[:, 0:1]).then_inc(ctl_words, 1)
                dve.wait_ge(ctl_step, 7 * n + 6)
                dve.tensor_copy(ctl[:, 0:1], cur[:, :]).then_inc(ctl_words, 1)
                dve.wait_ge(ctl_words, 2 * n + 2)
                dve.wait_ge(ctl_step, 7 * n + 7)
                dve.sem_inc(ctl_ready, 1)
                dve.load(regs, ctl[0:1, 0:4])

            dve.sem_inc(ctl_read, 1)
            next_step(0)
            publish(0)
            with dve.While(lambda: dve.snap(regs[0]) < LAYERS):
                dve.reg_add(steps_done, steps_done, 1)
                with dve.If(dve.snap(regs[2]) > 0):
                    a = dve.snap(attns)
                    dve.wait_ge(w_in, dve.snap(steps_done) * 48)
                    for q in range(PAIRS):
                        s = slice(C * q, C * q + C)
                        dve.tensor_copy(wbd[s, :, s], wat[s, :].rearrange("p (w n) -> p w n", w=4)).then_inc(bd_ready, 1)
                    dve.wait_ge(qkv_done, 3 * a + 2)
                    dve.tensor_copy(ks, bank(1)).then_inc(k_ready, 1)

                    def maxima(q):
                        dve.wait_ge(score_done, PAIRS * a + q + 1)
                        m = slice(4 * q, 4 * q + 4)
                        dve.tensor_reduce(mx[:, m], bank(4 + 2 * (q % 2), 2).rearrange("p (c k) -> p c k", c=4),
                                          AX.X, ALU.max).then_inc(attn_step, 1)
                        dve.wait_ge(attn_step, 8 * a + 2 * q + 1)
                        dve.tensor_scalar(nm[:, m], mx[:, m], -SCALE, None, ALU.mult).then_inc(max_ready, 1)

                    def heads(q):
                        m = slice(4 * q, 4 * q + 4)
                        dve.wait_ge(exp_done, 16 * a + 4 * q + 4)
                        dve.reciprocal(ri[:, m], sm[:, m]).then_inc(attn_step, 1)
                        dve.wait_ge(attn_step, 8 * a + 2 * q + 2)
                        dve.wait_ge(probT_done, PAIRS * a + q + 1)
                        dve.tensor_copy(pt[q % 2], bank(2, 2)).then_inc(probT_ready, 1)
                        dve.wait_ge(pv_done, PAIRS * a + q + 1)
                        dve.tensor_tensor(on.rearrange("p (c q d) -> p c q d", c=4, q=PAIRS)[:, :, q, :],
                                          bank(0).rearrange("p (c q d) -> p c q d", c=4, q=PAIRS)[:, :, q, :],
                                          ri[:, m].unsqueeze(2).broadcast_to([128, 4, C]), ALU.mult)\
                           .then_inc(head_ready, 1)

                    for q in range(PAIRS):
                        maxima(q)
                        heads(q)
                    dve.wait_ge(headT_done, a + 1)
                    dve.tensor_copy(ot, bank(1)).then_inc(headT_ready, 1)
                    dve.wait_ge(attn_out, a + 1)
                    dve.tensor_copy(h[:, :], bank(0)).then_inc(h_ready, 1)
                    dve.reg_add(attns, attns, 1)
                with dve.If(dve.snap(regs[3]) > 0):
                    f = dve.snap(ffns)
                    dve.wait_ge(w_in, dve.snap(steps_done) * 48)
                    for q in range(2, PAIRS):
                        dve.wait_ge(up_done, PAIRS * f + q + 1)
                        dve.tensor_scalar(hid[:, q, :], bank(4 + q), wdn[:, C:C + 1], 0.0, ALU.add, ALU.max)\
                           .then_inc(dve_relu, 1)
                    dve.wait_ge(down_done, f + 1)
                    dve.tensor_scalar(h[:, :], bank(0), wup[:, HID:HID + 1], None, ALU.add).then_inc(h_ready, 1)
                    dve.reg_add(ffns, ffns, 1)
                k = dve.snap(steps_done)
                next_step(k)
                publish(k)

            dve.wait_ge(h_ready, 1 + dve.snap(attns) + dve.snap(ffns))
            dve.tensor_tensor(fin[:, :], t2[:, :], h[:, :], ALU.add).then_inc(fin_ready, 1)

        @block.tensor
        def _(pe):
            def quad(q):
                return slice(C * q, C * q + C)

            pe.wait_ge(offw_in, 16)
            pe.wait_ge(xn_ready, 2)
            for t in range(TAPS):
                dy, dx = divmod(t, 3)
                ins = pe.matmul(bank(2), offw[:, t * 128:(t + 1) * 128], xpad[:, :, dy:dy + SIDE, dx:dx + SIDE],
                                start=t == 0, stop=t == TAPS - 1)
            ins.then_inc(off_done, 1)

            def filters(n):
                half, side = divmod(n, 2)
                if n:
                    pe.wait_ge(z_ready, n)
                for q in range(PAIRS):
                    px = xn[quad(q), half * HW + side * 128:half * HW + side * 128 + 128]
                    ins = pe.matmul(bank(3 + q)[:, 0:TAPS * C], px, convw[quad(q), :], start=True, stop=True)
                ins.then_inc(z_done, 1)

            pe.wait_ge(convw_in, 16)
            pe.wait_ge(xn_ready, HALVES + 1)
            filters(0)
            pe.wait_ge(const_in, 16)
            pe.wait_ge(off_ready, 1)
            for c in range(4):
                ins = pe.transpose(bank(1)[:, c * 128:(c + 1) * 128], off[:, c * 128:(c + 1) * 128], ident)
            ins.then_inc(offT_done, 1)
            for n in range(1, 4):
                filters(n)

            pe.wait_ge(x_in, 16 * HALVES)
            pe.matmul(bank(0), ident, xq[:, :], start=True, stop=False)
            pe.wait_ge(z_ready, 4)
            pe.sem_inc(samp_turned, 6)

            def turn(it, j):
                pe.wait_ge(samp_made[j], it + 1)
                for side in range(2):
                    s = 2 * j + side
                    pe.wait_ge(turned_ready, 6 * it + s + 1)
                    for q in range(2):
                        for hh in range(2):
                            for t in range(2):
                                at = q * BANK + hh * HW + t * 128
                                ins = pe.transpose(bank(2 + 2 * (s % 3), 2)[:, at:at + 128],
                                                   samp[j][:, 4 * t + 2 * side + q, hh * 128:hh * 128 + 128], ident)
                    ins.then_inc(samp_turned, 1)

            def tap_sum(it, half, j):
                pe.wait_ge(zk_ready, 3 * it + j + 1)
                pe.wait_ge(turned_ready, 6 * it + 2 * j + 2 + 3)
                for hh in range(2):
                    for q in range(PAIRS):
                        ins = pe.matmul(bank(0)[quad(q), half * HW:(half + 1) * HW], zk[j][:, q, hh, :],
                                        sampT[j][:, q, hh, :], start=False, stop=False)
                ins.then_inc(chunk_summed, 1)

            for half in range(HALVES):
                with pe.Fori(0, CHUNK_IT) as kk:
                    it = kk + CHUNK_IT * half
                    turn(it, 0)
                    turn(it, 1)
                    tap_sum(it, half, 0)
                    turn(it, 2)
                    tap_sum(it, half, 1)
                    tap_sum(it, half, 2)
            pe.wait_ge(zero_set, 1)

            def close(at, inc=None):
                ins = pe.matmul(at, zero_bf[:, 0:128], zero_bf[:, :], start=False, stop=True)
                if inc is not None:
                    ins.then_inc(inc, 1)

            close(bank(0), conv_done)

            def layer_norm(n, src):
                pe.wait_ge(ln_in, n + 1)
                pe.matmul(bank(1), part["average"], src[:, :], start=True, stop=True).then_inc(ln_mean, 1)
                pe.wait_ge(ln_sq, n + 1)
                pe.matmul(bank(1), part["average"], sq[:, :], start=True, stop=True).then_inc(ln_var, 1)

            layer_norm(0, t1)

            pe.wait_ge(ssmw_in, 16)
            pe.wait_ge(ln_out, 1)
            for s in range(2):
                for half in range(HALVES):
                    for q in range(PAIRS):
                        ins = pe.matmul(bank(q)[DI * half:DI * half + DI, s * HW:(s + 1) * HW],
                                        wt["w_in"][quad(q), s * DI:(s + 1) * DI], tn[quad(q), half * HW:(half + 1) * HW],
                                        start=True, stop=True)
            ins.then_inc(xz_done, 1)
            pe.wait_ge(xs_ready, 1)
            for name, at in (("w_delta", 4), ("w_b", 6), ("regroup", 2), ("w_c", 0)):
                if at == 2:
                    pe.wait_ge(gate_ready, 1)
                for c in range(2):
                    ins = pe.matmul(bank(at + c), wt[name], xs[:, c * BANK:(c + 1) * BANK], start=True, stop=True)
                ins.then_inc(dbc_done, 1)

            pe.wait_ge(picks_ready, 1)
            pe.wait_ge(stack_in, 16 * 2 * 3 * GROUPS)
            pe.wait_ge(part_rest[1], 1)
            pe.wait_ge(xg_ready, 1)
            pe.wait_ge(bx_ready, 1)
            pe.wait_ge(delta_ready, 1)
            for c in range(2):
                pe.matmul(bank(c), zero_bf[:, 0:128], zero_bf[:, :], start=True, stop=False)

            def spread_row(t, g, j, at):
                sel = picks[:, bass.ds(j * 128, 128)]
                for c in range(2):
                    ins = pe.matmul(bank(at + c), sel, stack[t][0:96, bass.ds(g * SEQ + c * BANK, BANK)],
                                    start=True, stop=True)
                return ins

            def add_product(r, stop):
                for c in range(2):
                    ins = pe.matmul(bank(c), ident, prod[r][:, c * BANK:(c + 1) * BANK], start=False, stop=stop)
                return ins

            with pe.Fori(0, GROUPS) as g:
                with pe.Fori(0, PER // 2) as jj:
                    for r in range(2):
                        n = PER * g + 2 * jj + r
                        pe.wait_ge(dbx_ready, n + 1)
                        spread_row(0, g, 2 * jj + r, 2 + 2 * r).then_inc(b_spread, 1)
                        pe.wait_ge(c_ready, n + 1)
                        spread_row(1, g, 2 * jj + r, 6).then_inc(c_spread, 1)
                        pe.wait_ge(prod_ready, n + 1)
                        add_product(r, False).then_inc(prod_summed, 1)
            for r in range(2):
                pe.wait_ge(prod_ready, DI + 1 + r)
                ins = add_product(r, r == 1)
            ins.then_inc(y_done, 1)

            pe.wait_ge(gated_ready, 1)
            for half in range(HALVES):
                s = slice(DI * half, DI * half + DI)
                for q in range(PAIRS):
                    ins = pe.matmul(bank(2 + half)[quad(q), 0:HW], wt["w_out"][s, :], gated[s, q * HW:(q + 1) * HW],
                                    start=True, stop=True)
            ins.then_inc(mix_done, 1)
            layer_norm(1, t2)

            regs = control_registers(pe, "pe")
            steps_done, attns, ffns = counters(pe, "pe")

            def first_token(n):
                pe.wait_ge(h_ready, n)
                pe.matmul(bank(3)[0:1, 0:32], h[:, 0:1], ident[:, 0:C], start=True, stop=True).then_inc(row_done, 1)

            first_token(1)
            pe.wait_ge(ctl_ready, 1)
            load_control(pe, regs)
            with pe.While(lambda: pe.snap(regs[0]) < LAYERS):
                pe.reg_add(steps_done, steps_done, 1)
                with pe.If(pe.snap(regs[2]) > 0):
                    a = pe.snap(attns)
                    pe.wait_ge(bd_ready, PAIRS * a + PAIRS)
                    for w in range(2):
                        pe.matmul(bank(w), wbd[:, w, :], h[:, :], start=True, stop=True).then_inc(qkv_done, 1)
                    for c in range(4):
                        ins = pe.matmul(bank(2)[:, c * 128:(c + 1) * 128], h[:, c * 128:(c + 1) * 128], wbd[:, 2, :],
                                        start=True, stop=True)
                    ins.then_inc(qkv_done, 1)
                    pe.wait_ge(qv_ready, 2 * a + 2)
                    pe.wait_ge(k_ready, a + 1)

                    def scores(q):
                        if q >= 2:
                            pe.wait_ge(exp_done, 16 * a + 4 * q - 4)
                        for half in range(HALVES):
                            for t in range(2):
                                c0 = half * HW + t * 128
                                ins = pe.matmul(bank(4 + 2 * (q % 2) + half)[:, t * HW:(t + 1) * HW],
                                                qs[quad(q), c0:c0 + 128], ks[quad(q), half * HW:(half + 1) * HW],
                                                start=True, stop=True)
                        ins.then_inc(score_done, 1)

                    def probabilities_times_values(q):
                        pe.wait_ge(exp_done, 16 * a + 4 * q + 4)
                        if q:
                            pe.wait_ge(probT_ready, PAIRS * a + q)
                        for half in range(HALVES):
                            for kt in range(2):
                                for t in range(2):
                                    at = ((half * 2 + kt) * 2 + t) * 128
                                    ins = pe.transpose(bank(2, 2)[:, at:at + 128],
                                                       es[q % 2][:, 2 * half + t, kt * 128:kt * 128 + 128], ident)
                        ins.then_inc(probT_done, 1)
                        pe.wait_ge(probT_ready, PAIRS * a + q + 1)
                        if q:
                            pe.wait_ge(head_ready, PAIRS * a + q)
                        for half in range(HALVES):
                            for t in range(2):
                                for kt in range(2):
                                    at = ((half * 2 + kt) * 2 + t) * 128
                                    c = 2 * half + t
                                    v0 = (2 * half + kt) * 128 + C * q
                                    ins = pe.matmul(bank(0)[:, c * 128 + C * q:c * 128 + C * q + C],
                                                    pt[q % 2][:, at:at + 128], vs[:, v0:v0 + C],
                                                    start=kt == 0, stop=kt == 1)
                        ins.then_inc(pv_done, 1)

                    scores(0)
                    for q in range(PAIRS):
                        if q + 1 < PAIRS:
                            scores(q + 1)
                        probabilities_times_values(q)
                    pe.wait_ge(head_ready, PAIRS * a + PAIRS)
                    for c in range(4):
                        ins = pe.transpose(bank(1)[:, c * 128:(c + 1) * 128], on[:, c * 128:(c + 1) * 128], ident)
                    ins.then_inc(headT_done, 1)
                    pe.wait_ge(headT_ready, a + 1)
                    pe.matmul(bank(0), wbd[:, 3, :], ot, start=True, stop=True).then_inc(attn_out, 1)
                    pe.reg_add(attns, attns, 1)
                with pe.If(pe.snap(regs[3]) > 0):
                    f = pe.snap(ffns)
                    pe.wait_ge(w_in, pe.snap(steps_done) * 48)
                    pe.wait_ge(h_ready, 1 + pe.snap(attns) + f)
                    for q in range(PAIRS):
                        pe.matmul(bank(4 + q), wup[quad(q), 0:HID], h[quad(q), :], start=True, stop=True)\
                          .then_inc(up_done, 1)
                    for q in range(PAIRS):
                        if q < 2:
                            pe.wait_ge(act_relu, 2 * f + q + 1)
                        else:
                            pe.wait_ge(dve_relu, 2 * f + q - 1)
                        ins = pe.matmul(bank(0)[quad(q), :], wdn[:, 0:C], hid[:, q, :], start=True, stop=True)
                    ins.then_inc(down_done, 1)
                    pe.reg_add(ffns, ffns, 1)
                first_token(1 + pe.snap(attns) + pe.snap(ffns))
                hold(pe, ctl_ready, pe.snap(steps_done) + 1)
                load_control(pe, regs)


def _constants(np):
    level = np.arange(SIDE, dtype=np.float32)
    grid = np.zeros((PAIRS, C, HALVES, SIDE, SIDE), np.float32)
    for k in range(TAPS):
        kh, kw = divmod(k, 3)
        grid[:, 2 * k] = (level - 1 + kh)[:, None]
        grid[:, 2 * k + 1] = (level - 1 + kw)[None, :]
    average = np.kron(np.eye(PAIRS, dtype=np.float32), np.full((C, C), 1.0 / C, np.float32))
    return {"level": np.tile(level, (128, 1)), "ident": np.eye(128, dtype=np.float32), "average": average,
            "grid": grid.reshape(128, TOK), "eps": np.full((128, 1), GN_EPS, np.float32),
            "pad": np.zeros((128, 1), np.float32)}


def _packed(np, where, width, parts):
    out = np.zeros((128, width), np.float32)
    for name, (a, b) in where.items():
        out[:, a:b] = parts[name]
    return out


def kernel(**inputs):
    import numpy as np
    import concourse.bacc as bacc
    import ml_dtypes
    from concourse.bass_utils import run_bass_kernel_spmd

    g = {k: np.asarray(v) for k, v in inputs.items()}

    def quad_rows(a):
        return np.tile(a, (PAIRS, 1))

    def block_diagonal(a, n):
        out = np.zeros((n, a.shape[0], n, a.shape[1]), a.dtype)
        for i in range(n):
            out[i, :, i] = a
        return out.reshape(n * a.shape[0], n * a.shape[1])

    def group_columns(a):
        bd = block_diagonal(a, HALVES).reshape(128, HALVES, GROUPS, PER)
        return bd.transpose(0, 2, 1, 3).reshape(128, 128)

    parts = _constants(np)
    off_b = np.zeros(C, np.float32)
    off_b[:OFFS] = g["L0_conv_offset_b"]
    parts["offset_b"] = quad_rows(off_b[:, None])
    parts["conv_b"] = quad_rows(g["L0_conv_bias"][:, None])
    ow = np.zeros((TAPS, C, C), np.float32)
    ow[:, :, :OFFS] = g["L0_conv_offset_w"].reshape(OFFS, C, TAPS).transpose(2, 1, 0)
    offset_w = np.concatenate([block_diagonal(w, PAIRS) for w in ow], axis=1)
    conv_w = quad_rows(g["L0_conv_weight"].reshape(C, C, TAPS).transpose(1, 2, 0).reshape(C, TAPS * C))
    ssm = {"w_in": quad_rows(g["L1_attn_W_in"]), "w_delta": block_diagonal(g["L1_attn_W_delta"], HALVES),
           "w_b": group_columns(g["L1_attn_W_B"]), "w_c": group_columns(g["L1_attn_W_C"]),
           "regroup": group_columns(np.eye(DI, dtype=np.float32)),
           "w_out": np.tile(g["L1_attn_W_out"], (HALVES, 1)), "a": np.tile(g["L1_attn_A"], (HALVES, 1))}
    steps = np.concatenate([np.arange(LAYERS), LAYERS - np.arange(LAYERS)]).astype(np.float32)[None]
    masks = np.stack([g["L1_ffn_attn_mask"].T, g["L1_ffn_ffn_mask"].T]).reshape(1, -1)
    n = LAYERS * OPS
    w_attn = np.concatenate([g[f"L1_ffn_{w}"].reshape(n, C, C) for w in ("wq", "wk", "wv", "wo")], axis=2)
    w_up = np.concatenate([g["L1_ffn_ffn_w1"].reshape(n, C, HID), g["L1_ffn_ffn_b2"].reshape(n, C, 1)], axis=2)
    w_down = np.concatenate([g["L1_ffn_ffn_w2"].reshape(n, HID, C), g["L1_ffn_ffn_b1"].reshape(n, HID, 1)], axis=2)
    arrays = {
        "x_dram": g["x"].reshape(B, C, HW),
        "const_dram": _packed(np, CONST, CONST_W, parts),
        "offset_w_dram": offset_w, "conv_w_dram": conv_w,
        "ssm_w_dram": _packed(np, SSM, SSM_W, ssm),
        "spread_dram": np.tile(np.eye(32, dtype=np.float32), (3, 1)).astype(ml_dtypes.bfloat16),
        "masks_dram": masks, "steps_dram": steps,
        "w_attn_dram": w_attn, "w_up_dram": w_up, "w_down_dram": w_down,
    }
    arrays = {k: np.ascontiguousarray(v) for k, v in arrays.items()}
    nc = bacc.Bacc("TRN2", target_bir_lowering=False, num_devices=1)
    aps = [nc.dram_tensor(k, a.shape, mybir.dt.from_np(a.dtype), kind="ExternalInput").ap() for k, a in arrays.items()]
    out = nc.dram_tensor("out_dram", (B, C, HW), mybir.dt.float32, kind="ExternalOutput").ap()
    aps[0] = aps[0].rearrange("(q b) c n -> b q c n", b=HALVES)
    hybrid_kernel(nc, *aps, out.rearrange("(q b) c n -> b q c n", b=HALVES))
    r = run_bass_kernel_spmd(nc, [arrays], core_ids=[0])
    return r.results[0]["out_dram"].reshape(B, C, SIDE, SIDE)
```

```python
from contextlib import ExitStack

import concourse.bass as bass
from concourse import mybir

B, C, HW = 8, 32, 256
SIDE = 16
PAIRS, HALVES = 4, 2
TAPS = 9
OFFS = 2 * TAPS
DI = 64
LAYERS, OPS, HID = 33, 19, 128
TOK = HALVES * HW
SEQ = PAIRS * HW
GN_EPS = 1e-5
BANK = 512
GROUPS, PER = 4, 16


def columns(sizes):
    at, out = 0, {}
    for name, size in sizes:
        out[name] = (at, at + size)
        at += size
    return out, at


CONST, CONST_W = columns([("offset_b", 1), ("conv_b", 1), ("eps", 1), ("pad", 1), ("level", SIDE), ("ident", 128),
                          ("average", 128), ("pairs", PAIRS), ("onehot", HALVES * (2 * PER - 1)), ("grid", TOK)])
SSM, SSM_W = columns([("w_xs", PAIRS * DI), ("w_delta", 128), ("w_b", 128), ("w_c", 128),
                      ("w_gate", PAIRS * HALVES * 128), ("w_out", HALVES * C), ("a", DI)])


def hybrid_kernel(nc, x, const, offset_w, conv_w, ssm_w, spread_w, masks, steps, w_attn, w_up, w_down, out):
    f32, bf16, i32, u32, u8 = (mybir.dt.float32, mybir.dt.bfloat16, mybir.dt.int32, mybir.dt.uint32, mybir.dt.uint8)
    ALU = mybir.AluOpType
    ACT = mybir.ActivationFunctionType
    AX = mybir.AxisListType
    SCALE = 1.0 / C ** 0.5

    ctx = ExitStack()
    with ctx:
        def sb(name, shape, dt=f32):
            return ctx.enter_context(nc.sbuf_tensor(name, shape, dt))

        def sem(name):
            return ctx.enter_context(nc.semaphore(name))

        cst = sb("cst", [128, CONST_W])
        offw = sb("offw", [128, TAPS * 128])
        convw = sb("convw", [128, TAPS * C])
        ssmw = sb("ssmw", [128, SSM_W])
        spread = sb("spread", [96, 32], bf16)
        picks = sb("picks", [96, PER * 128], bf16)
        zero_bf = sb("zero_bf", [128, BANK], bf16)
        part = {n: cst[:, a:b] for n, (a, b) in CONST.items()}
        wt = {n: ssmw[:, a:b] for n, (a, b) in SSM.items()}
        ident = part["ident"]

        xq = sb("xq", [128, TOK])
        t1 = sb("t1", [128, TOK])
        t2 = sb("t2", [128, TOK])
        cen = sb("cen", [128, TOK])
        sq = sb("sq", [128, TOK])
        root = sb("root", [128, 16])
        inv = sb("inv", [128, 16])
        inv_wide = sb("inv_wide", [128, TOK])
        tn = sb("tn", [128, TOK])
        h = sb("h", [128, TOK])
        fin = sb("fin", [128, TOK])
        unused = sb("unused", [128, 1])
        stats = sb("stats", [128, HALVES, 6])
        mv = sb("mv", [128, HALVES, 2])
        gsd = sb("gsd", [128, HALVES])
        grs = sb("grs", [128, HALVES])

        pool = sb("pool", [128, 31 * 1024])
        used = {"conv": 0, "ssm": 0, "ffn": 0}

        def region(phase, n):
            a = used[phase]
            used[phase] = a + n
            assert used[phase] <= 31 * 1024
            return pool[:, a:a + n]

        PADDED = SIDE + 2
        HATS = 8 * 6 * SIDE
        xpad = region("conv", HALVES * PADDED * PADDED).rearrange("p (b y x) -> p b y x", b=HALVES, y=PADDED)
        xn = region("conv", TOK)
        off = region("conv", TOK)
        hat = region("conv", 8 * HATS).rearrange("p (i c o y) -> p i c o y", i=8, c=8, o=6)
        zs = region("conv", 16 * TAPS * C).rearrange("p (b q h k) -> p b q h k", b=HALVES, q=PAIRS, h=2)
        samp = [region("conv", 8 * HW).rearrange("p (c n) -> p c n", c=8) for _ in range(3)]
        sampT = [region("conv", 8 * HW).rearrange("p (q h n) -> p q h n", q=PAIRS, h=2) for _ in range(3)]
        zk = [region("conv", 8 * C).rearrange("p (q h o) -> p q h o", q=PAIRS, h=2) for _ in range(3)]

        xs = region("ssm", SEQ)
        th = region("ssm", SEQ)
        gate = region("ssm", SEQ)
        bx = region("ssm", SEQ)
        cn = region("ssm", SEQ)
        rest = region("ssm", SEQ)
        pieces = [region("ssm", SEQ // 2).bitcast(bf16) for _ in range(3)]
        stack = region("ssm", GROUPS * SEQ // 2).bitcast(bf16)
        dA = [region("ssm", SEQ) for _ in range(GROUPS)]
        dbx = [region("ssm", SEQ) for _ in range(GROUPS)]
        state = [region("ssm", SEQ) for _ in range(GROUPS)]
        prod = [region("ssm", SEQ) for _ in range(2 * GROUPS)]
        pick = [region("ssm", HALVES * PER) for _ in range(2)]
        gated = region("ssm", SEQ)

        wat = region("ffn", 128)
        wbd = region("ffn", 4 * 128).rearrange("p (w n) -> p w n", w=4)
        wup = region("ffn", HID + 1)
        region("ffn", 3)
        wdn = region("ffn", C + 1)
        region("ffn", 3)
        qs, ks, vs, on, ot = (region("ffn", TOK) for _ in range(5))
        es = [region("ffn", 1024).rearrange("p (c k) -> p c k", c=4) for _ in range(2)]
        pt = [region("ffn", 1024) for _ in range(2)]
        mx = region("ffn", 16)
        nm = region("ffn", 16)
        sm = region("ffn", 16)
        ri = region("ffn", 16)
        hid = region("ffn", PAIRS * TOK).rearrange("p (q n) -> p q n", q=PAIRS)
        row = sb("row", [1, 32])
        top = sb("top", [1, 8])
        idx = sb("idx", [1, 8], u32)
        mask8 = sb("mask8", [1, 2 * OPS * LAYERS], u8)
        stepno = sb("stepno", [1, 2 * LAYERS])
        tab = sb("tab", [1, OPS * 3 * LAYERS])
        cand = sb("cand", [1, 3 * LAYERS])
        best = sb("best", [1, 4])
        cur = sb("cur", [1, 1])
        ctl = sb("ctl", [1, 4], i32)

        ps = ctx.enter_context(nc.psum_tensor("ps", [128, 8 * BANK], f32))

        def bank(i, n=1):
            return ps[:, i * BANK:(i + n) * BANK]

        x_in, const_in, offw_in, convw_in, ssmw_in, spread_in, ctl_in = map(
            sem, ["x_in", "const_in", "offw_in", "convw_in", "ssmw_in", "spread_in", "ctl_in"])
        picks_ready, hat_abs = sem("picks_ready"), sem("hat_abs")
        pad_zeroed, zero_set, wbd_zeroed = map(sem, ["pad_zeroed", "zero_set", "wbd_zeroed"])
        dve_step, act_step, pool_step = map(sem, ["dve_step", "act_step", "pool_step"])
        gn_var, gn_sd, xn_ready = map(sem, ["gn_var", "gn_sd", "xn_ready"])
        off_done, off_ready, offT_done, hat_diff, hat_ready = map(
            sem, ["off_done", "off_ready", "offT_done", "hat_diff", "hat_ready"])
        z_done, z_ready = map(sem, ["z_done", "z_ready"])
        samp_made = [sem(f"samp_made{j}") for j in range(3)]
        samp_turned, turned_ready, zk_ready, chunk_summed, conv_done = map(
            sem, ["samp_turned", "turned_ready", "zk_ready", "chunk_summed", "conv_done"])
        ln_in, ln_mean, ln_cen, ln_sq, ln_var, ln_sd, ln_out = map(
            sem, ["ln_in", "ln_mean", "ln_cen", "ln_sq", "ln_var", "ln_sd", "ln_out"])
        ln_inv, ln_turned = sem("ln_inv"), sem("ln_turned")
        delta_done, xs_done, b_done, gate_in_done, c_done = map(
            sem, ["delta_done", "xs_done", "b_done", "gate_in_done", "c_done"])
        xs_ready, th_ready, gate_ready = map(sem, ["xs_ready", "th_ready", "gate_ready"])
        part_cast, part_rest, bx_ready, c_ready = map(sem, ["part_cast", "part_rest", "bx_ready", "c_ready"])
        stack_in = [sem(f"stack_in{g}") for g in range(GROUPS)]
        delta_spread, da_ready, dbx_ready, scanned, prod_ready, pick_ready, prod_summed, y_done = map(
            sem, ["delta_spread", "da_ready", "dbx_ready", "scanned", "prod_ready", "pick_ready", "prod_summed",
                  "y_done"])
        gated_ready, mix_done, da_zeroed = map(sem, ["gated_ready", "mix_done", "da_zeroed"])
        h_ready, row_done, ctl_step, ctl_words, ctl_ready, ctl_read, held, w_in = map(
            sem, ["h_ready", "row_done", "ctl_step", "ctl_words", "ctl_ready", "ctl_read", "held", "w_in"])
        bd_ready, qkv_done, qv_ready, k_ready, score_done, max_ready, exp_done, probT_done, probT_ready = map(
            sem, ["bd_ready", "qkv_done", "qv_ready", "k_ready", "score_done", "max_ready", "exp_done", "probT_done",
                  "probT_ready"])
        pv_done, head_ready, headT_done, headT_ready, attn_out, attn_step = map(
            sem, ["pv_done", "head_ready", "headT_done", "headT_ready", "attn_out", "attn_step"])
        up_done, act_relu, dve_relu, down_done = map(sem, ["up_done", "act_relu", "dve_relu", "down_done"])
        fin_ready, out_stored = map(sem, ["fin_ready", "out_stored"])

        block = ctx.enter_context(nc.Block())

        ROWS = 3

        def sampling_chunk(eng, it, j):
            eng.wait_ge(hat_ready, it + 1)
            eng.wait_ge(samp_turned, 6 * it + 2 * j + 2)
            now = hat[:, bass.ds(it, 1), :, 2 * j:2 * j + 2, :].rearrange("p i c o y -> p (i c) o y")
            eng.tensor_tensor(samp[j].rearrange("p c (y x) -> p c y x", y=SIDE),
                              now[:, :, 0, :].unsqueeze(3).broadcast_to([128, 8, SIDE, SIDE]),
                              now[:, :, 1, :].unsqueeze(2).broadcast_to([128, 8, SIDE, SIDE]),
                              ALU.mult).then_inc(samp_made[j], 1)

        def hold(eng, semaphore, value):
            eng.wait_ge(semaphore, value)
            eng.sem_inc(held, 1)

        def load_control(eng, regs):
            eng.load(regs, ctl[0:1, 0:4])
            eng.sem_inc(ctl_read, 1)

        def control_registers(eng, tag):
            return [eng.alloc_register(f"{tag}_{n}") for n in ("layer", "op", "attn", "ffn")]

        def counters(eng, tag):
            regs = [eng.alloc_register(f"{tag}_{n}") for n in ("steps", "attns", "ffns")]
            for r in regs:
                eng.reg_mov(r, 0)
            return regs

        @block.sync
        def _(sp):
            for half in range(HALVES):
                sp.dma_start(xq[:, half * HW:(half + 1) * HW], x[half]).then_inc(x_in, 16)
            sp.dma_start(cst[:, :], const).then_inc(const_in, 16)
            sp.dma_start(convw[:, :], conv_w).then_inc(convw_in, 16)
            sp.dma_start(ssmw[:, :], ssm_w).then_inc(ssmw_in, 16)
            sp.dma_start(spread[:, :], spread_w).then_inc(spread_in, 16)
            sp.dma_start(mask8[:, :], masks).then_inc(ctl_in, 16)
            sp.dma_start(stepno[:, :], steps).then_inc(ctl_in, 16)

            for p in range(3):
                sp.wait_ge(part_cast, p + 1)
                for g in range(GROUPS):
                    sp.dma_start(stack[32 * p:32 * p + 32, g * SEQ:(g + 1) * SEQ],
                                 pieces[p][32 * g:32 * g + 32, :]).then_inc(stack_in[g], 16)

            regs = control_registers(sp, "sp")
            steps_done, _, _ = counters(sp, "sp")
            layer, op = regs[0], regs[1]
            sp.wait_ge(ctl_ready, 1)
            load_control(sp, regs)
            with sp.While(lambda: sp.snap(layer) < LAYERS):
                sp.reg_add(steps_done, steps_done, 1)
                at = sp.snap(sp.snap(layer) * OPS + sp.snap(op), min_val=0, max_val=LAYERS * OPS - 1)
                sp.dma_start(wup, w_up[bass.ds(at, 1), :, :].rearrange("o c n -> (o c) n").unsqueeze(0)
                             .broadcast_to([PAIRS, C, HID + 1])).then_inc(w_in, 16)
                sp.dma_start(wdn, w_down[bass.ds(at, 1), :, :].rearrange("o c n -> (o c) n")).then_inc(w_in, 16)
                sp.dma_start(wat, w_attn[bass.ds(at, 1), :, :].rearrange("o c n -> (o c) n").unsqueeze(0)
                             .broadcast_to([PAIRS, C, 128])).then_inc(w_in, 16)
                hold(sp, ctl_ready, sp.snap(steps_done) + 1)
                load_control(sp, regs)

            sp.wait_ge(fin_ready, 1)
            for half in range(HALVES):
                sp.dma_start(out[half], fin[:, half * HW:(half + 1) * HW]).then_inc(out_stored, 16)
            sp.wait_ge(out_stored, 16 * HALVES)

        @block.gpsimd
        def _(pool_e):
            pool_e.memset(xpad, 0.0).then_inc(pad_zeroed, 1)
            pool_e.memset(zero_bf[:, :], 0.0).then_inc(zero_set, 1)
            pool_e.sem_inc(chunk_summed, 3)
            pool_e.wait_ge(spread_in, 16)
            pool_e.tensor_copy(picks[:, :].rearrange("p (j b d) -> p b j d", j=PER, b=HALVES),
                               spread[:, :].rearrange("p (b j) -> p b j", b=HALVES).unsqueeze(3)
                               .broadcast_to([96, HALVES, PER, DI])).then_inc(picks_ready, 1)

            with pool_e.Fori(0, ROWS) as kk:
                for half in range(HALVES):
                    it = HALVES * kk + half
                    sampling_chunk(pool_e, it, 2)
                    pool_e.wait_ge(z_ready, 4)
                    for j in range(3):
                        k = 3 * kk + j
                        pool_e.wait_ge(chunk_summed, 3 * it + j + 1)
                        pool_e.tensor_copy(zk[j], zs[:, half, :, :, bass.ds(k * C, C)]).then_inc(zk_ready, 1)

            pool_e.wait_ge(conv_done, 1)
            for t in range(GROUPS):
                pool_e.memset(dA[t], 0.0).then_inc(da_zeroed, 1)
            for t in range(2 * GROUPS):
                pool_e.memset(prod[t], 0.0).then_inc(pool_step, 1)
            for t in range(2):
                pool_e.memset(pick[t], 0.0).then_inc(pool_step, 1)
            pool_e.wait_ge(pool_step, 2 * GROUPS + 2)
            pool_e.sem_inc(prod_ready, GROUPS)
            pool_e.sem_inc(pick_ready, 1)
            pool_e.wait_ge(c_ready, 1)
            with pool_e.Fori(0, PER // 2) as it:
                for jp in range(2):
                    pool_e.wait_ge(prod_summed, 2 * it + jp + 1)
                    for g in range(GROUPS):
                        e = 8 * it + GROUPS * jp + g
                        pool_e.wait_ge(scanned, e + GROUPS + 1)
                        pool_e.tensor_tensor(prod[GROUPS * jp + g], state[g], cn, ALU.mult).then_inc(prod_ready, 1)

        @block.scalar
        def _(act):
            act.dma_start(offw[:, :], offset_w).then_inc(offw_in, 16)
            act.wait_ge(const_in, 16)
            act.wait_ge(gn_var, 2)
            act.activation(gsd[:, :], mv[:, :, 1], ACT.Sqrt, bias=part["eps"]).then_inc(gn_sd, 1)

            act.sem_inc(turned_ready, 3)

            def evacuate_filters(n):
                act.wait_ge(z_done, n + 1)
                half, side = divmod(n, 2)
                act.activation(zs[:, half, :, side, :], bank(3, 4).rearrange("p (q k) -> p q k", q=PAIRS)
                               [:, :, 0:TAPS * C], ACT.Copy).then_inc(z_ready, 1)

            def hats(i):
                act.wait_ge(hat_abs, i + 1)
                v = hat[:, bass.ds(i, 1), :, :, :].rearrange("p i c o y -> p (i c o y)")
                act.activation(v, v, ACT.Relu, bias=1.0, scale=-1.0).then_inc(hat_ready, 1)

            evacuate_filters(0)
            evacuate_filters(1)
            hats(0)
            evacuate_filters(2)
            hats(1)
            evacuate_filters(3)

            with act.Fori(0, ROWS) as kk:
                for half in range(HALVES):
                    it = HALVES * kk + half
                    for j in range(3):
                        act.wait_ge(chunk_summed, 3 * it + j + 1)
                        for side in range(2):
                            s = 2 * j + side
                            act.wait_ge(samp_turned, 6 * it + s + 7)
                            act.activation(sampT[j][:, 2 * side:2 * side + 2].rearrange("p q h n -> p (q h n)"),
                                           bank(2 + 2 * (s % 3), 2), ACT.Copy).then_inc(turned_ready, 1)
                        if j == 1:
                            hats(it + HALVES)

            def bring_in(function):
                act.activation(unused[:, :], part["eps"], function).then_inc(act_step, 1)
                act.wait_ge(act_step, tables.pop(0))

            tables = [1, 2]

            def layer_norm(n):
                act.wait_ge(ln_cen, n + 1)
                act.activation(sq[:, :], cen[:, :], ACT.Square).then_inc(ln_sq, 1)
                act.wait_ge(ln_var, n + 1)
                act.activation(root[:, :], bank(1)[:, 0:16], ACT.Sqrt, bias=part["eps"]).then_inc(ln_sd, 1)

            layer_norm(0)
            act.wait_ge(xs_done, 1)
            act.activation(xs, bank(4, 2), ACT.Copy).then_inc(xs_ready, 1)
            bring_in(ACT.Exp)
            act.wait_ge(delta_done, 1)
            act.activation(pieces[0], bank(2, 2), ACT.Copy).then_inc(part_cast, 1)
            act.wait_ge(part_rest, 1)
            act.activation(pieces[1], rest, ACT.Copy).then_inc(part_cast, 1)
            act.wait_ge(gate_in_done, 1)
            act.activation(th, bank(6, 2), ACT.Tanh, scale=0.5).then_inc(th_ready, 1)
            act.wait_ge(c_done, 1)
            act.activation(cn, bank(4, 2), ACT.Copy).then_inc(c_ready, 1)

            act.wait_ge(da_zeroed, GROUPS)
            act.sem_inc(da_ready, 2)

            def inner_tail(ap):
                return ap.rearrange("p (q n) -> p q n", q=PAIRS)[:, :, 1:HW]

            onehot = part["onehot"].rearrange("p (b w) -> p b w", b=HALVES)
            with act.Fori(0, PER // 2) as it:
                for jp in range(2):
                    j = 2 * it + jp
                    for g in range(GROUPS):
                        e = 8 * it + GROUPS * jp + g
                        act.wait_ge(delta_spread, e + 1)
                        act.wait_ge(scanned, e + 1)
                        act.activation(inner_tail(dA[g]), inner_tail(bank(2 + 2 * (g % 2), 2)), ACT.Exp,
                                       scale=wt["a"][:, bass.ds(PER * g + j, 1)]).then_inc(da_ready, 1)
                    act.wait_ge(prod_summed, j + 1)
                    act.activation(pick[jp].rearrange("p (b w) -> p b w", b=HALVES),
                                   onehot[:, :, bass.ds(PER - 1 - j, PER)], ACT.Copy).then_inc(pick_ready, 1)

            bring_in(ACT.Sqrt)
            layer_norm(1)

            regs = control_registers(act, "act")
            steps_done, attns, ffns = counters(act, "act")
            act.wait_ge(ctl_ready, 1)
            load_control(act, regs)
            with act.While(lambda: act.snap(regs[0]) < LAYERS):
                act.reg_add(steps_done, steps_done, 1)
                with act.If(act.snap(regs[2]) > 0):
                    a = act.snap(attns)
                    act.wait_ge(qkv_done, 3 * a + 1)
                    act.activation(qs, bank(0), ACT.Copy).then_inc(qv_ready, 1)
                    act.wait_ge(qkv_done, 3 * a + 3)
                    act.activation(vs, bank(2), ACT.Copy).then_inc(qv_ready, 1)
                    for q in range(PAIRS):
                        act.wait_ge(max_ready, PAIRS * a + q + 1)
                        if q >= 2:
                            act.wait_ge(probT_done, PAIRS * a + q - 1)
                        for c in range(4):
                            i = 4 * q + c
                            act.activation(es[q % 2][:, c, :], bank(4 + 2 * (q % 2), 2)[:, c * HW:(c + 1) * HW],
                                           ACT.Exp, bias=nm[:, i:i + 1], scale=SCALE,
                                           accum_out=sm[:, i:i + 1]).then_inc(exp_done, 1)
                    act.reg_add(attns, attns, 1)
                with act.If(act.snap(regs[3]) > 0):
                    f = act.snap(ffns)
                    act.wait_ge(w_in, act.snap(steps_done) * 48)
                    for q in range(2):
                        act.wait_ge(up_done, PAIRS * f + q + 1)
                        act.activation(hid[:, q, :], bank(4 + q), ACT.Relu, bias=wdn[:, C:C + 1]).then_inc(act_relu, 1)
                    act.reg_add(ffns, ffns, 1)
                hold(act, ctl_ready, act.snap(steps_done) + 1)
                load_control(act, regs)

        @block.vector
        def _(dve):
            made = [0]

            def step(ins):
                ins.then_inc(dve_step, 1)
                made[0] += 1

            def settle():
                dve.wait_ge(dve_step, made[0])

            dve.wait_ge(x_in, 16 * HALVES)
            for half in range(HALVES):
                step(dve.bn_stats(stats[:, half, :], xq[:, half * HW:(half + 1) * HW]))
            settle()
            for half in range(HALVES):
                dve.bn_aggr(mv[:, half, :], stats[:, half, :]).then_inc(gn_var, 1)
            dve.wait_ge(gn_sd, 1)
            step(dve.reciprocal(grs[:, :], gsd[:, :]))
            settle()
            dve.wait_ge(gn_var, 2)
            dve.wait_ge(pad_zeroed, 1)
            for half in range(HALVES):
                dve.tensor_scalar(xpad[:, half, 1:1 + SIDE, 1:1 + SIDE],
                                  xq[:, half * HW:(half + 1) * HW].rearrange("p (y x) -> p y x", y=SIDE),
                                  mv[:, half, 0:1], grs[:, half:half + 1], ALU.subtract, ALU.mult)\
                   .then_inc(xn_ready, 1)
            dve.wait_ge(xn_ready, HALVES)
            dve.tensor_copy(xn.rearrange("p (b y x) -> p b y x", b=HALVES, y=SIDE),
                            xpad[:, :, 1:1 + SIDE, 1:1 + SIDE]).then_inc(xn_ready, 1)

            dve.wait_ge(off_done, 1)
            dve.wait_ge(const_in, 16)
            dve.scalar_tensor_tensor(off, bank(2), part["offset_b"], part["grid"], ALU.add, ALU.add)\
               .then_inc(off_ready, 1)
            def distances(half, kk):
                i = HALVES * kk + half
                pos = bank(1)[:, half * HW:(half + 1) * HW].rearrange("p (c o) -> p c o", c=8)[:, :, bass.ds(6 * kk, 6)]
                v = hat[:, bass.ds(i, 1), :, :, :].rearrange("p i c o y -> p (i c) o y")
                dve.tensor_tensor(v, pos.unsqueeze(3).broadcast_to([128, 8, 6, SIDE]),
                                  part["level"].unsqueeze(1).unsqueeze(1).broadcast_to([128, 8, 6, SIDE]),
                                  ALU.subtract).then_inc(hat_diff, 1)
                dve.wait_ge(hat_diff, i + 1)
                flat = v.rearrange("p c o y -> p (c o y)")
                dve.scalar_tensor_tensor(flat, flat, -1.0, flat, ALU.mult, ALU.max).then_inc(hat_abs, 1)

            dve.wait_ge(offT_done, 1)
            for half in range(HALVES):
                distances(half, 0)
            with dve.Fori(0, ROWS) as kk:
                for half in range(HALVES):
                    for j in range(2):
                        sampling_chunk(dve, HALVES * kk + half, j)
                    distances(half, kk + 1)

            dve.wait_ge(conv_done, 1)
            dve.tensor_scalar(t1[:, :], bank(0), part["conv_b"], None, ALU.add).then_inc(ln_in, 1)

            def layer_norm(n, src, dst):
                dve.wait_ge(ln_in, n + 1)
                dve.wait_ge(ln_mean, n + 1)
                dve.tensor_tensor(cen[:, :], src[:, :], bank(1), ALU.subtract).then_inc(ln_cen, 1)
                dve.wait_ge(ln_sd, n + 1)
                step(dve.reciprocal(inv[:, :], root[:, :]))
                settle()
                dve.tensor_copy(inv_wide[:, :].rearrange("p (k c) -> p k c", k=16),
                                inv[:, :].unsqueeze(2).broadcast_to([128, 16, C])).then_inc(ln_inv, 1)
                dve.wait_ge(ln_turned, n + 1)
                return dve.tensor_tensor(dst[:, :], cen[:, :], bank(1), ALU.mult)

            layer_norm(0, t1, tn).then_inc(ln_out, 1)

            dve.wait_ge(ctl_in, 32)
            tabv = tab[:, :].rearrange("p (o s l) -> p o s l", o=OPS, s=3)
            m8 = mask8[:, :].rearrange("p (s o l) -> p s o l", s=2, o=OPS)
            left = stepno[:, LAYERS:2 * LAYERS].unsqueeze(1).broadcast_to([1, OPS, LAYERS])
            for s in range(2):
                step(dve.tensor_tensor(tabv[:, :, 1 + s, :], m8[:, s, :, :], left, ALU.mult))
            settle()
            step(dve.tensor_tensor(tabv[:, :, 0, :], tabv[:, :, 1, :], tabv[:, :, 2, :], ALU.max))
            step(dve.memset(cur[:, :], -1.0))

            dve.wait_ge(part_cast, 1)
            dve.tensor_tensor(rest, bank(2, 2), pieces[0], ALU.subtract).then_inc(part_rest, 1)
            dve.wait_ge(part_cast, 2)
            dve.tensor_tensor(pieces[2], rest, pieces[1], ALU.subtract).then_inc(part_cast, 1)
            dve.wait_ge(xs_ready, 1)
            dve.wait_ge(b_done, 1)
            dve.tensor_tensor(bx, xs, bank(0, 2), ALU.mult).then_inc(bx_ready, 1)
            dve.wait_ge(th_ready, 1)
            dve.scalar_tensor_tensor(gate, th, 1.0, bank(6, 2), ALU.add, ALU.mult).then_inc(gate_ready, 1)

            dve.wait_ge(bx_ready, 1)
            dve.sem_inc(dbx_ready, 2)
            dve.sem_inc(scanned, GROUPS)
            with dve.Fori(0, PER // 2) as it:
                def added(i):
                    e = 8 * it + i
                    dve.wait_ge(da_ready, e + 3)
                    dve.wait_ge(scanned, e + 1)
                    dve.tensor_tensor(dbx[i % GROUPS], bx, bank(2 + 2 * (i % 2), 2), ALU.mult).then_inc(dbx_ready, 1)

                def scan(i):
                    e = 8 * it + i
                    dve.wait_ge(dbx_ready, e + 3)
                    dve.wait_ge(prod_ready, e + 1)
                    dve.tensor_tensor_scan(state[i % GROUPS], dA[i % GROUPS], dbx[i % GROUPS], 0.0, ALU.mult, ALU.add)\
                       .then_inc(scanned, 1)

                added(0)
                for i in range(1, 2 * GROUPS):
                    added(i)
                    scan(i - 1)
                scan(2 * GROUPS - 1)

            dve.wait_ge(y_done, 1)
            dve.wait_ge(gate_ready, 1)
            dve.scalar_tensor_tensor(gated, bank(0, 2), 0.5, gate, ALU.mult, ALU.mult).then_inc(gated_ready, 1)
            dve.wait_ge(mix_done, 1)
            for half in range(HALVES):
                ins = dve.tensor_tensor(t2[:, half * HW:(half + 1) * HW], t1[:, half * HW:(half + 1) * HW],
                                        bank(2)[:, half * HW:(half + 1) * HW], ALU.add)
                if half:
                    ins.then_inc(ln_in, 1)
                else:
                    step(ins)
            settle()
            layer_norm(1, t2, h).then_inc(h_ready, 1)
            step(dve.memset(wbd, 0.0))
            settle()

            regs = control_registers(dve, "dve")
            steps_done, attns, ffns = counters(dve, "dve")
            op_reg = dve.alloc_register("dve_chosen")

            def next_step(n):
                dve.wait_ge(row_done, n + 1)
                c = 7 * n
                dve.tensor_copy(row[:, :], bank(3)[0:1, 0:32]).then_inc(ctl_step, 1)
                hold(dve, ctl_step, c + 1)
                dve.max(top[:, :], row[:, 0:OPS]).then_inc(ctl_step, 1)
                hold(dve, ctl_step, c + 2)
                dve.max_index(idx[:, :], top[:, :], row[:, 0:OPS]).then_inc(ctl_step, 1)
                hold(dve, ctl_step, c + 3)
                dve.load([op_reg], idx[0:1, 0:1])
                op = dve.snap(op_reg, min_val=0, max_val=OPS - 1)
                v = cand[:, :].rearrange("p (s l) -> p s l", s=3)
                dve.scalar_tensor_tensor(v, stepno[:, 0:LAYERS].unsqueeze(1).broadcast_to([1, 3, LAYERS]), cur[:, 0:1],
                                         tab[:, bass.ds(op * (3 * LAYERS), 3 * LAYERS)]
                                         .rearrange("p (s l) -> p s l", s=3), ALU.is_gt, ALU.mult).then_inc(ctl_step, 1)
                dve.wait_ge(ctl_step, c + 4)
                dve.tensor_reduce(best[:, 0:3], v, AX.X, ALU.max).then_inc(ctl_step, 1)
                dve.wait_ge(ctl_step, c + 5)
                dve.tensor_scalar(cur[:, :], best[:, 0:1], -1.0, float(LAYERS), ALU.mult, ALU.add).then_inc(ctl_step, 1)
                dve.wait_ge(ctl_read, 3 * n + 1)
                dve.tensor_scalar(ctl[:, 2:4], best[:, 1:3], best[:, 0:1], None, ALU.is_equal).then_inc(ctl_step, 1)

            def publish(n):
                dve.tensor_copy(ctl[:, 1:2], idx[:, 0:1]).then_inc(ctl_words, 1)
                dve.wait_ge(ctl_step, 7 * n + 6)
                dve.tensor_copy(ctl[:, 0:1], cur[:, :]).then_inc(ctl_words, 1)
                dve.wait_ge(ctl_words, 2 * n + 2)
                dve.wait_ge(ctl_step, 7 * n + 7)
                dve.sem_inc(ctl_ready, 1)
                dve.load(regs, ctl[0:1, 0:4])

            dve.sem_inc(ctl_read, 1)
            next_step(0)
            publish(0)
            with dve.While(lambda: dve.snap(regs[0]) < LAYERS):
                dve.reg_add(steps_done, steps_done, 1)
                with dve.If(dve.snap(regs[2]) > 0):
                    a = dve.snap(attns)
                    dve.wait_ge(w_in, dve.snap(steps_done) * 48)
                    for q in range(PAIRS):
                        s = slice(C * q, C * q + C)
                        dve.tensor_copy(wbd[s, :, s], wat[s, :].rearrange("p (w n) -> p w n", w=4)).then_inc(bd_ready, 1)
                    dve.wait_ge(qkv_done, 3 * a + 2)
                    dve.tensor_copy(ks, bank(1)).then_inc(k_ready, 1)

                    chain = [0]

                    def attention_step(ins):
                        ins.then_inc(attn_step, 1)
                        chain[0] += 1
                        dve.wait_ge(attn_step, 8 * a + chain[0])

                    def maxima(q):
                        dve.wait_ge(score_done, PAIRS * a + q + 1)
                        m = slice(4 * q, 4 * q + 4)
                        attention_step(dve.tensor_reduce(mx[:, m], bank(4 + 2 * (q % 2), 2)
                                                         .rearrange("p (c k) -> p c k", c=4), AX.X, ALU.max))
                        dve.tensor_scalar(nm[:, m], mx[:, m], -SCALE, None, ALU.mult).then_inc(max_ready, 1)

                    def heads(q):
                        m = slice(4 * q, 4 * q + 4)
                        dve.wait_ge(exp_done, 16 * a + 4 * q + 4)
                        attention_step(dve.reciprocal(ri[:, m], sm[:, m]))
                        dve.wait_ge(probT_done, PAIRS * a + q + 1)
                        dve.tensor_copy(pt[q % 2], bank(2, 2)).then_inc(probT_ready, 1)
                        dve.wait_ge(pv_done, PAIRS * a + q + 1)
                        dve.tensor_tensor(on.rearrange("p (c q d) -> p c q d", c=4, q=PAIRS)[:, :, q, :],
                                          bank(0).rearrange("p (c q d) -> p c q d", c=4, q=PAIRS)[:, :, q, :],
                                          ri[:, m].unsqueeze(2).broadcast_to([128, 4, C]), ALU.mult)\
                           .then_inc(head_ready, 1)

                    maxima(0)
                    maxima(1)
                    for q in range(PAIRS):
                        heads(q)
                        if q + 2 < PAIRS:
                            maxima(q + 2)
                    dve.wait_ge(headT_done, a + 1)
                    dve.tensor_copy(ot, bank(1)).then_inc(headT_ready, 1)
                    dve.wait_ge(attn_out, a + 1)
                    dve.tensor_copy(h[:, :], bank(0)).then_inc(h_ready, 1)
                    dve.reg_add(attns, attns, 1)
                with dve.If(dve.snap(regs[3]) > 0):
                    f = dve.snap(ffns)
                    dve.wait_ge(w_in, dve.snap(steps_done) * 48)
                    for q in range(2, PAIRS):
                        dve.wait_ge(up_done, PAIRS * f + q + 1)
                        dve.tensor_scalar(hid[:, q, :], bank(4 + q), wdn[:, C:C + 1], 0.0, ALU.add, ALU.max)\
                           .then_inc(dve_relu, 1)
                    dve.wait_ge(down_done, f + 1)
                    dve.tensor_scalar(h[:, :], bank(0), wup[:, HID:HID + 1], None, ALU.add).then_inc(h_ready, 1)
                    dve.reg_add(ffns, ffns, 1)
                k = dve.snap(steps_done)
                next_step(k)
                publish(k)

            dve.wait_ge(h_ready, 1 + dve.snap(attns) + dve.snap(ffns))
            dve.tensor_tensor(fin[:, :], t2[:, :], h[:, :], ALU.add).then_inc(fin_ready, 1)

        @block.tensor
        def _(pe):
            def quad(q):
                return slice(C * q, C * q + C)

            def offset_taps(taps):
                for t in taps:
                    dy, dx = divmod(t, 3)
                    ins = pe.matmul(bank(2), offw[:, t * 128:(t + 1) * 128], xpad[:, :, dy:dy + SIDE, dx:dx + SIDE],
                                    start=t == 0, stop=t == TAPS - 1)
                return ins

            def filters(n):
                half, side = divmod(n, 2)
                if n:
                    pe.wait_ge(z_ready, n)
                for q in range(PAIRS):
                    px = xn[quad(q), half * HW + side * 128:half * HW + side * 128 + 128]
                    ins = pe.matmul(bank(3 + q)[:, 0:TAPS * C], px, convw[quad(q), :], start=True, stop=True)
                ins.then_inc(z_done, 1)

            pe.sem_inc(samp_turned, 6)
            pe.wait_ge(offw_in, 16)
            pe.wait_ge(xn_ready, HALVES)
            offset_taps(range(0, 3))
            pe.wait_ge(convw_in, 16)
            pe.wait_ge(xn_ready, HALVES + 1)
            filters(0)
            offset_taps(range(3, 6))
            filters(1)
            offset_taps(range(6, TAPS)).then_inc(off_done, 1)
            pe.wait_ge(const_in, 16)
            pe.wait_ge(off_ready, 1)
            for c in range(4):
                ins = pe.transpose(bank(1)[:, c * 128:(c + 1) * 128], off[:, c * 128:(c + 1) * 128], ident)
            ins.then_inc(offT_done, 1)
            for n in range(2, 4):
                filters(n)

            pe.wait_ge(x_in, 16 * HALVES)
            pe.matmul(bank(0), ident, xq[:, :], start=True, stop=False)
            pe.wait_ge(z_ready, 4)

            def turn(it, j):
                pe.wait_ge(samp_made[j], it + 1)
                for side in range(2):
                    s = 2 * j + side
                    pe.wait_ge(turned_ready, 6 * it + s + 1)
                    for q in range(2):
                        for hh in range(2):
                            for t in range(2):
                                at = q * BANK + hh * HW + t * 128
                                ins = pe.transpose(bank(2 + 2 * (s % 3), 2)[:, at:at + 128],
                                                   samp[j][:, 4 * t + 2 * side + q, hh * 128:hh * 128 + 128], ident)
                    ins.then_inc(samp_turned, 1)

            def tap_sum(it, half, j):
                pe.wait_ge(zk_ready, 3 * it + j + 1)
                pe.wait_ge(turned_ready, 6 * it + 2 * j + 2 + 3)
                for hh in range(2):
                    for q in range(PAIRS):
                        ins = pe.matmul(bank(0)[quad(q), half * HW:(half + 1) * HW], zk[j][:, q, hh, :],
                                        sampT[j][:, q, hh, :], start=False, stop=False)
                ins.then_inc(chunk_summed, 1)

            with pe.Fori(0, ROWS) as kk:
                chunks = [(HALVES * kk + half, half, j) for half in range(HALVES) for j in range(3)]
                for n, (it, half, j) in enumerate(chunks):
                    turn(it, j)
                    if n:
                        tap_sum(*chunks[n - 1])
                tap_sum(*chunks[-1])
            pe.wait_ge(zero_set, 1)

            def close(at, inc=None):
                ins = pe.matmul(at, zero_bf[:, 0:128], zero_bf[:, :], start=False, stop=True)
                if inc is not None:
                    ins.then_inc(inc, 1)

            close(bank(0), conv_done)

            def layer_norm(n, src):
                pe.wait_ge(ln_in, n + 1)
                pe.matmul(bank(1), part["average"], src[:, :], start=True, stop=True).then_inc(ln_mean, 1)
                pe.wait_ge(ln_sq, n + 1)
                for c in range(4):
                    ins = pe.matmul(bank(1)[:, PAIRS * c:PAIRS * (c + 1)], sq[:, c * 128:(c + 1) * 128], part["pairs"],
                                    start=True, stop=True)
                ins.then_inc(ln_var, 1)
                pe.wait_ge(ln_inv, n + 1)
                for c in range(4):
                    ins = pe.transpose(bank(1)[:, c * 128:(c + 1) * 128], inv_wide[:, c * 128:(c + 1) * 128], ident)
                ins.then_inc(ln_turned, 1)

            layer_norm(0, t1)

            def project(at, weights, inc):
                for c in range(2):
                    ins = pe.matmul(bank(at + c), weights, xs[:, c * BANK:(c + 1) * BANK], start=True, stop=True)
                ins.then_inc(inc, 1)

            pe.wait_ge(ssmw_in, 16)
            pe.wait_ge(ln_out, 1)
            for q in range(PAIRS):
                for half in range(HALVES):
                    ins = pe.matmul(bank(4, 2)[DI * half:DI * half + DI, q * HW:(q + 1) * HW],
                                    wt["w_xs"][:, q * DI:(q + 1) * DI], tn[:, half * HW:(half + 1) * HW],
                                    start=True, stop=True)
            ins.then_inc(xs_done, 1)

            def gate_input(q):
                for half in range(HALVES):
                    at = (HALVES * q + half) * 128
                    ins = pe.matmul(bank(6, 2)[:, q * HW:(q + 1) * HW], wt["w_gate"][:, at:at + 128],
                                    tn[:, half * HW:(half + 1) * HW], start=half == 0, stop=half == 1)
                return ins

            gate_input(0)
            pe.wait_ge(xs_ready, 1)
            project(2, wt["w_delta"], delta_done)
            project(0, wt["w_b"], b_done)
            for q in range(1, PAIRS):
                ins = gate_input(q)
            ins.then_inc(gate_in_done, 1)
            project(4, wt["w_c"], c_done)

            pe.wait_ge(picks_ready, 1)
            pe.wait_ge(bx_ready, 1)
            for c in range(2):
                pe.matmul(bank(c), zero_bf[:, 0:128], zero_bf[:, :], start=True, stop=False)
            pe.wait_ge(c_ready, 1)
            pe.wait_ge(prod_ready, GROUPS)
            pe.wait_ge(pick_ready, 1)

            def add_products(jp, c, stop=False):
                for g in range(GROUPS):
                    ins = pe.matmul(bank(c)[quad(g), :], pick[jp], prod[GROUPS * jp + g][:, c * BANK:(c + 1) * BANK],
                                    start=False, stop=stop)
                return ins

            with pe.Fori(0, PER // 2) as it:
                for jp in range(2):
                    j = 2 * it + jp
                    for g in range(GROUPS):
                        e = 8 * it + GROUPS * jp + g
                        pe.wait_ge(stack_in[g], 16 * 3)
                        pe.wait_ge(da_ready, e + 1)
                        pe.wait_ge(dbx_ready, e + 1)
                        for c in range(2):
                            ins = pe.matmul(bank(2 + 2 * (g % 2) + c), picks[:, bass.ds(j * 128, 128)],
                                            stack[0:96, g * SEQ + c * BANK:g * SEQ + (c + 1) * BANK],
                                            start=True, stop=True)
                        ins.then_inc(delta_spread, 1)
                        if g == 0:
                            add_products(jp, 1).then_inc(prod_summed, 1)
                    pe.wait_ge(prod_ready, GROUPS * j + GROUPS)
                    pe.wait_ge(pick_ready, j + 1)
                    add_products(1 - jp, 0)
            add_products(0, 1)
            pe.wait_ge(prod_ready, DI + GROUPS)
            pe.wait_ge(pick_ready, PER + 1)
            add_products(1, 0, True)
            add_products(1, 1, True).then_inc(y_done, 1)

            pe.wait_ge(gated_ready, 1)
            for half in range(HALVES):
                for q in range(PAIRS):
                    ins = pe.matmul(bank(2)[quad(q), half * HW:(half + 1) * HW], wt["w_out"][:, half * C:(half + 1) * C],
                                    gated[:, q * HW:(q + 1) * HW], start=True, stop=True)
            ins.then_inc(mix_done, 1)
            layer_norm(1, t2)

            regs = control_registers(pe, "pe")
            steps_done, attns, ffns = counters(pe, "pe")

            def first_token(n):
                pe.wait_ge(h_ready, n)
                pe.matmul(bank(3)[0:1, 0:32], h[:, 0:1], ident[:, 0:C], start=True, stop=True).then_inc(row_done, 1)

            first_token(1)
            pe.wait_ge(ctl_ready, 1)
            load_control(pe, regs)
            with pe.While(lambda: pe.snap(regs[0]) < LAYERS):
                pe.reg_add(steps_done, steps_done, 1)
                with pe.If(pe.snap(regs[2]) > 0):
                    a = pe.snap(attns)
                    pe.wait_ge(bd_ready, PAIRS * a + PAIRS)
                    for w in range(2):
                        pe.matmul(bank(w), wbd[:, w, :], h[:, :], start=True, stop=True).then_inc(qkv_done, 1)
                    for c in range(4):
                        ins = pe.matmul(bank(2)[:, c * 128:(c + 1) * 128], h[:, c * 128:(c + 1) * 128], wbd[:, 2, :],
                                        start=True, stop=True)
                    ins.then_inc(qkv_done, 1)
                    pe.wait_ge(qv_ready, 2 * a + 2)
                    pe.wait_ge(k_ready, a + 1)

                    def scores(q):
                        if q >= 2:
                            pe.wait_ge(exp_done, 16 * a + 4 * q - 4)
                        for half in range(HALVES):
                            for t in range(2):
                                c0 = half * HW + t * 128
                                ins = pe.matmul(bank(4 + 2 * (q % 2) + half)[:, t * HW:(t + 1) * HW],
                                                qs[quad(q), c0:c0 + 128], ks[quad(q), half * HW:(half + 1) * HW],
                                                start=True, stop=True)
                        ins.then_inc(score_done, 1)

                    def turn_probabilities(q):
                        pe.wait_ge(exp_done, 16 * a + 4 * q + 4)
                        if q:
                            pe.wait_ge(probT_ready, PAIRS * a + q)
                        for half in range(HALVES):
                            for kt in range(2):
                                for t in range(2):
                                    at = ((half * 2 + kt) * 2 + t) * 128
                                    ins = pe.transpose(bank(2, 2)[:, at:at + 128],
                                                       es[q % 2][:, 2 * half + t, kt * 128:kt * 128 + 128], ident)
                        ins.then_inc(probT_done, 1)

                    def probabilities_times_values(q):
                        pe.wait_ge(probT_ready, PAIRS * a + q + 1)
                        if q:
                            pe.wait_ge(head_ready, PAIRS * a + q)
                        for half in range(HALVES):
                            for t in range(2):
                                for kt in range(2):
                                    at = ((half * 2 + kt) * 2 + t) * 128
                                    c = 2 * half + t
                                    v0 = (2 * half + kt) * 128 + C * q
                                    ins = pe.matmul(bank(0)[:, c * 128 + C * q:c * 128 + C * q + C],
                                                    pt[q % 2][:, at:at + 128], vs[:, v0:v0 + C],
                                                    start=kt == 0, stop=kt == 1)
                        ins.then_inc(pv_done, 1)

                    scores(0)
                    scores(1)
                    for q in range(PAIRS):
                        turn_probabilities(q)
                        if q + 2 < PAIRS:
                            scores(q + 2)
                        probabilities_times_values(q)
                    pe.wait_ge(head_ready, PAIRS * a + PAIRS)
                    for c in range(4):
                        ins = pe.transpose(bank(1)[:, c * 128:(c + 1) * 128], on[:, c * 128:(c + 1) * 128], ident)
                    ins.then_inc(headT_done, 1)
                    pe.wait_ge(headT_ready, a + 1)
                    pe.matmul(bank(0), wbd[:, 3, :], ot, start=True, stop=True).then_inc(attn_out, 1)
                    pe.reg_add(attns, attns, 1)
                with pe.If(pe.snap(regs[3]) > 0):
                    f = pe.snap(ffns)
                    pe.wait_ge(w_in, pe.snap(steps_done) * 48)
                    pe.wait_ge(h_ready, 1 + pe.snap(attns) + f)
                    for q in range(PAIRS):
                        pe.matmul(bank(4 + q), wup[quad(q), 0:HID], h[quad(q), :], start=True, stop=True)\
                          .then_inc(up_done, 1)
                    for q in range(PAIRS):
                        if q < 2:
                            pe.wait_ge(act_relu, 2 * f + q + 1)
                        else:
                            pe.wait_ge(dve_relu, 2 * f + q - 1)
                        ins = pe.matmul(bank(0)[quad(q), :], wdn[:, 0:C], hid[:, q, :], start=True, stop=True)
                    ins.then_inc(down_done, 1)
                    pe.reg_add(ffns, ffns, 1)
                first_token(1 + pe.snap(attns) + pe.snap(ffns))
                hold(pe, ctl_ready, pe.snap(steps_done) + 1)
                load_control(pe, regs)


def _constants(np):
    level = np.arange(SIDE, dtype=np.float32)
    grid = np.zeros((PAIRS, C, HALVES, SIDE, SIDE), np.float32)
    for k in range(TAPS):
        kh, kw = divmod(k, 3)
        grid[:, 2 * k] = (level - 1 + kh)[:, None]
        grid[:, 2 * k + 1] = (level - 1 + kw)[None, :]
    average = np.kron(np.eye(PAIRS, dtype=np.float32), np.full((C, C), 1.0 / C, np.float32))
    pairs = np.kron(np.eye(PAIRS, dtype=np.float32), np.full((C, 1), 1.0 / C, np.float32))
    onehot = np.zeros((HALVES, DI, HALVES, 2 * PER - 1), np.float32)
    for half in range(HALVES):
        onehot[half, :, half, PER - 1] = 1.0
    return {"pairs": pairs, "onehot": onehot.reshape(128, -1), "level": np.tile(level, (128, 1)), "ident": np.eye(128, dtype=np.float32), "average": average,
            "grid": grid.reshape(128, TOK), "eps": np.full((128, 1), GN_EPS, np.float32),
            "pad": np.zeros((128, 1), np.float32)}


def _packed(np, where, width, parts):
    out = np.zeros((128, width), np.float32)
    for name, (a, b) in where.items():
        out[:, a:b] = parts[name]
    return out


def kernel(**inputs):
    import numpy as np
    import concourse.bacc as bacc
    import ml_dtypes
    from concourse.bass_utils import run_bass_kernel_spmd

    g = {k: np.asarray(v) for k, v in inputs.items()}

    def quad_rows(a):
        return np.tile(a, (PAIRS, 1))

    def block_diagonal(a, n):
        out = np.zeros((n, a.shape[0], n, a.shape[1]), a.dtype)
        for i in range(n):
            out[i, :, i] = a
        return out.reshape(n * a.shape[0], n * a.shape[1])

    def group_columns(a):
        bd = block_diagonal(a, HALVES).reshape(128, HALVES, GROUPS, PER)
        return bd.transpose(0, 2, 1, 3).reshape(128, 128)

    parts = _constants(np)
    off_b = np.zeros(C, np.float32)
    off_b[:OFFS] = g["L0_conv_offset_b"]
    parts["offset_b"] = quad_rows(off_b[:, None])
    parts["conv_b"] = quad_rows(g["L0_conv_bias"][:, None])
    ow = np.zeros((TAPS, C, C), np.float32)
    ow[:, :, :OFFS] = g["L0_conv_offset_w"].reshape(OFFS, C, TAPS).transpose(2, 1, 0)
    offset_w = np.concatenate([block_diagonal(w, PAIRS) for w in ow], axis=1)
    conv_w = quad_rows(g["L0_conv_weight"].reshape(C, C, TAPS).transpose(1, 2, 0).reshape(C, TAPS * C))
    w_out = np.zeros((GROUPS, HALVES, PER, HALVES, C), np.float32)
    for half in range(HALVES):
        w_out[:, half, :, half] = g["L1_attn_W_out"].reshape(GROUPS, PER, C)
    w_in = g["L1_attn_W_in"]
    w_gate = np.zeros((C, HALVES, GROUPS, HALVES, PER), np.float32)
    for half in range(HALVES):
        w_gate[:, half, :, half] = w_in[:, DI:].reshape(C, GROUPS, PER)
    ssm = {"w_xs": block_diagonal(w_in[:, :DI], PAIRS), "w_delta": group_columns(g["L1_attn_W_delta"]),
           "w_b": block_diagonal(g["L1_attn_W_B"], HALVES), "w_c": block_diagonal(g["L1_attn_W_C"], HALVES),
           "w_gate": block_diagonal(w_gate.reshape(C, -1), PAIRS),
           "w_out": w_out.reshape(128, HALVES * C), "a": np.tile(g["L1_attn_A"].T, (HALVES, 1))}
    steps = np.concatenate([np.arange(LAYERS), LAYERS - np.arange(LAYERS)]).astype(np.float32)[None]
    masks = np.stack([g["L1_ffn_attn_mask"].T, g["L1_ffn_ffn_mask"].T]).reshape(1, -1)
    n = LAYERS * OPS
    w_attn = np.concatenate([g[f"L1_ffn_{w}"].reshape(n, C, C) for w in ("wq", "wk", "wv", "wo")], axis=2)
    w_up = np.concatenate([g["L1_ffn_ffn_w1"].reshape(n, C, HID), g["L1_ffn_ffn_b2"].reshape(n, C, 1)], axis=2)
    w_down = np.concatenate([g["L1_ffn_ffn_w2"].reshape(n, HID, C), g["L1_ffn_ffn_b1"].reshape(n, HID, 1)], axis=2)
    arrays = {
        "x_dram": g["x"].reshape(B, C, HW),
        "const_dram": _packed(np, CONST, CONST_W, parts),
        "offset_w_dram": offset_w, "conv_w_dram": conv_w,
        "ssm_w_dram": _packed(np, SSM, SSM_W, ssm),
        "spread_dram": np.tile(np.eye(32, dtype=np.float32), (3, 1)).astype(ml_dtypes.bfloat16),
        "masks_dram": masks, "steps_dram": steps,
        "w_attn_dram": w_attn, "w_up_dram": w_up, "w_down_dram": w_down,
    }
    arrays = {k: np.ascontiguousarray(v) for k, v in arrays.items()}
    nc = bacc.Bacc("TRN2", target_bir_lowering=False, num_devices=1)
    aps = [nc.dram_tensor(k, a.shape, mybir.dt.from_np(a.dtype), kind="ExternalInput").ap() for k, a in arrays.items()]
    out = nc.dram_tensor("out_dram", (B, C, HW), mybir.dt.float32, kind="ExternalOutput").ap()
    aps[0] = aps[0].rearrange("(q b) c n -> b q c n", b=HALVES)
    hybrid_kernel(nc, *aps, out.rearrange("(q b) c n -> b q c n", b=HALVES))
    r = run_bass_kernel_spmd(nc, [arrays], core_ids=[0])
    return r.results[0]["out_dram"].reshape(B, C, SIDE, SIDE)
```

```python
from contextlib import ExitStack

import concourse.bass as bass
from concourse import mybir

B, C, HW = 8, 32, 256
SIDE = 16
PAIRS, HALVES = 4, 2
TAPS = 9
OFFS = 2 * TAPS
DI = 64
LAYERS, OPS, HID = 33, 19, 128
TOK = HALVES * HW
SEQ = PAIRS * HW
GN_EPS = 1e-5
BANK = 512
GROUPS, PER = 4, 16


def columns(sizes):
    at, out = 0, {}
    for name, size in sizes:
        out[name] = (at, at + size)
        at += size
    return out, at


CONST, CONST_W = columns([("offset_b", 1), ("conv_b", 1), ("level", SIDE), ("ident", 128),
                          ("centre", 128), ("pairs", PAIRS), ("onehot", HALVES * (2 * PER - 1)), ("grid", TOK)])
SSM, SSM_W = columns([("w_xs", PAIRS * DI), ("w_delta", 128), ("w_b", 128), ("w_c", 128),
                      ("w_gate", PAIRS * HALVES * 128), ("w_out", HALVES * C), ("a", DI)])


def hybrid_kernel(nc, x, const, offset_w, conv_w, ssm_w, spread_w, masks, steps, w_attn, w_up, w_down, out):
    f32, bf16, i32, u32, u8 = (mybir.dt.float32, mybir.dt.bfloat16, mybir.dt.int32, mybir.dt.uint32, mybir.dt.uint8)
    ALU = mybir.AluOpType
    ACT = mybir.ActivationFunctionType
    AX = mybir.AxisListType
    SCALE = 1.0 / C ** 0.5

    ctx = ExitStack()
    with ctx:
        def sb(name, shape, dt=f32):
            return ctx.enter_context(nc.sbuf_tensor(name, shape, dt))

        def sem(name):
            return ctx.enter_context(nc.semaphore(name))

        cst = sb("cst", [128, CONST_W])
        offw = sb("offw", [128, TAPS * 128])
        convw = sb("convw", [128, TAPS * C])
        ssmw = sb("ssmw", [128, SSM_W])
        spread = sb("spread", [96, 32], bf16)
        picks = sb("picks", [96, PER * 128], bf16)
        zero_bf = sb("zero_bf", [128, BANK], bf16)
        part = {n: cst[:, a:b] for n, (a, b) in CONST.items()}
        wt = {n: ssmw[:, a:b] for n, (a, b) in SSM.items()}
        ident = part["ident"]

        xq = sb("xq", [128, TOK])
        t1 = sb("t1", [128, TOK])
        t2 = sb("t2", [128, TOK])
        cen = sb("cen", [128, TOK])
        sq = sb("sq", [128, TOK])
        root = sb("root", [128, 16])
        inv = sb("inv", [128, 16])
        inv_wide = sb("inv_wide", [128, TOK])
        tn = sb("tn", [128, TOK])
        h = sb("h", [128, TOK])
        fin = sb("fin", [128, TOK])
        unused = sb("unused", [128, 3])
        ones = sb("ones", [128, 1])
        eps = sb("eps", [128, 1])
        stats = sb("stats", [128, HALVES, 6])
        mv = sb("mv", [128, HALVES, 2])
        gsd = sb("gsd", [128, HALVES])
        grs = sb("grs", [128, HALVES])

        pool = sb("pool", [128, 31 * 1024])
        used = {"conv": 0, "ssm": 0, "ffn": 0}

        def region(phase, n):
            a = used[phase]
            used[phase] = a + n
            assert used[phase] <= 31 * 1024
            return pool[:, a:a + n]

        PADDED = SIDE + 2
        HATS = 8 * 6 * SIDE
        xpad = region("conv", HALVES * PADDED * PADDED).rearrange("p (b y x) -> p b y x", b=HALVES, y=PADDED)
        xn = region("conv", TOK)
        off = region("conv", TOK)
        hat = region("conv", 8 * HATS).rearrange("p (i c o y) -> p i c o y", i=8, c=8, o=6)
        zs = region("conv", 16 * TAPS * C).rearrange("p (b q h k) -> p b q h k", b=HALVES, q=PAIRS, h=2)
        samp = [region("conv", 8 * HW).rearrange("p (c n) -> p c n", c=8) for _ in range(3)]
        sampT = [region("conv", 8 * HW).rearrange("p (q h n) -> p q h n", q=PAIRS, h=2) for _ in range(3)]
        zk = [region("conv", 8 * C).rearrange("p (q h o) -> p q h o", q=PAIRS, h=2) for _ in range(3)]

        xs = region("ssm", SEQ)
        gate = region("ssm", SEQ)
        bx = region("ssm", SEQ)
        cn = region("ssm", SEQ)
        rest = region("ssm", SEQ)
        pieces = [region("ssm", SEQ // 2).bitcast(bf16) for _ in range(3)]
        stack = region("ssm", GROUPS * SEQ // 2).bitcast(bf16)
        dA = [region("ssm", SEQ) for _ in range(GROUPS)]
        dbx = [region("ssm", SEQ) for _ in range(GROUPS)]
        state = [region("ssm", SEQ) for _ in range(GROUPS)]
        prod = [region("ssm", SEQ) for _ in range(2 * GROUPS)]
        pick = [region("ssm", HALVES * PER) for _ in range(2)]
        gated = region("ssm", SEQ)

        wat = region("ffn", 128)
        wup = region("ffn", HID + 4)[:, 0:HID + 1]
        wdn = region("ffn", C + 4)[:, 0:C + 1]
        qs, ks, vs, ot, ri_wide, ri_turned = (region("ffn", TOK) for _ in range(6))
        es = [region("ffn", 1024).rearrange("p (c k) -> p c k", c=4) for _ in range(2)]
        pt = [region("ffn", 1024) for _ in range(2)]
        mx = region("ffn", 16)
        nm = region("ffn", 16)
        sm = region("ffn", 16)
        ri = region("ffn", 16)
        hid = region("ffn", PAIRS * TOK).rearrange("p (q n) -> p q n", q=PAIRS)
        wbd = sb("wbd", [128, 4, 128])
        top = sb("top", [1, 8])
        idx = sb("idx", [1, 8], u32)
        mask8 = sb("mask8", [1, 2 * OPS * LAYERS], u8)
        stepno = sb("stepno", [1, 2 * LAYERS])
        tab = sb("tab", [1, OPS * 3 * LAYERS])
        cand = sb("cand", [1, 3 * LAYERS])
        best = sb("best", [1, 4])
        cur = sb("cur", [1, 1])
        ctl = sb("ctl", [1, 4], i32)

        ps = ctx.enter_context(nc.psum_tensor("ps", [128, 8 * BANK], f32))

        def bank(i, n=1):
            return ps[:, i * BANK:(i + n) * BANK]

        x_in, const_in, offw_in, convw_in, ssmw_in, spread_in, ctl_in = map(
            sem, ["x_in", "const_in", "offw_in", "convw_in", "ssmw_in", "spread_in", "ctl_in"])
        picks_ready, hat_abs = sem("picks_ready"), sem("hat_abs")
        pad_zeroed, zero_set, wbd_zeroed = map(sem, ["pad_zeroed", "zero_set", "wbd_zeroed"])
        dve_step, act_step, prod_zeroed = map(sem, ["dve_step", "act_step", "prod_zeroed"])
        gn_var, gn_sd, xn_ready = map(sem, ["gn_var", "gn_sd", "xn_ready"])
        off_done, off_ready, offT_done, hat_diff, hat_ready = map(
            sem, ["off_done", "off_ready", "offT_done", "hat_diff", "hat_ready"])
        z_done, z_ready = map(sem, ["z_done", "z_ready"])
        samp_made = [sem(f"samp_made{j}") for j in range(3)]
        samp_turned, turned_ready, zk_ready, chunk_summed, conv_done = map(
            sem, ["samp_turned", "turned_ready", "zk_ready", "chunk_summed", "conv_done"])
        ln_in, ln_cen, ln_sq, ln_var, ln_sd, ln_out = map(
            sem, ["ln_in", "ln_cen", "ln_sq", "ln_var", "ln_sd", "ln_out"])
        ln_inv, ln_turned = sem("ln_inv"), sem("ln_turned")
        delta_done, xs_done, b_done, gate_in_done, c_done = map(
            sem, ["delta_done", "xs_done", "b_done", "gate_in_done", "c_done"])
        xs_ready, gate_ready = sem("xs_ready"), sem("gate_ready")
        part_rest, bx_ready, c_ready = map(sem, ["part_rest", "bx_ready", "c_ready"])
        part_ready = [sem(f"part_ready{p}") for p in range(3)]
        stack_in = [sem(f"stack_in{g}") for g in range(GROUPS)]
        delta_spread, da_ready, dbx_ready, scanned, prod_ready, pick_ready, prod_summed, y_done = map(
            sem, ["delta_spread", "da_ready", "dbx_ready", "scanned", "prod_ready", "pick_ready", "prod_summed",
                  "y_done"])
        gated_ready, mix_done, da_zeroed, last_prod_ready, table_input = map(
            sem, ["gated_ready", "mix_done", "da_zeroed", "last_prod_ready", "table_input"])
        eps_set = sem("eps_set")
        late_scanned, late_prod_ready = sem("late_scanned"), sem("late_prod_ready")
        h_ready, row_done, ctl_step, ctl_words, ctl_ready, ctl_read, held = map(
            sem, ["h_ready", "row_done", "ctl_step", "ctl_words", "ctl_ready", "ctl_read", "held"])
        w_attn_in, w_up_in, w_down_in = sem("w_attn_in"), sem("w_up_in"), sem("w_down_in")
        bd_ready, qkv_done, qv_ready, k_ready, score_done, max_ready, exp_done, probT_done, probT_ready = map(
            sem, ["bd_ready", "qkv_done", "qv_ready", "k_ready", "score_done", "max_ready", "exp_done", "probT_done",
                  "probT_ready"])
        pv_done, ri_wide_ready, ri_turn_done, ri_turned_ready, head_ready, attn_out, attn_step = map(
            sem, ["pv_done", "ri_wide_ready", "ri_turn_done", "ri_turned_ready", "head_ready", "attn_out", "attn_step"])
        relu_table, exp_table = sem("relu_table"), sem("exp_table")
        up_done, act_relu, dve_relu, down_done = map(sem, ["up_done", "act_relu", "dve_relu", "down_done"])
        fin_ready, out_stored = map(sem, ["fin_ready", "out_stored"])

        block = ctx.enter_context(nc.Block())

        ROWS = 3

        def sampling_chunk(eng, it, j):
            eng.wait_ge(hat_ready, it + 1)
            eng.wait_ge(samp_turned, 6 * it + 2 * j + 2)
            now = hat[:, bass.ds(it, 1), :, 2 * j:2 * j + 2, :].rearrange("p i c o y -> p (i c) o y")
            eng.tensor_tensor(samp[j].rearrange("p c (y x) -> p c y x", y=SIDE),
                              now[:, :, 0, :].unsqueeze(3).broadcast_to([128, 8, SIDE, SIDE]),
                              now[:, :, 1, :].unsqueeze(2).broadcast_to([128, 8, SIDE, SIDE]),
                              ALU.mult).then_inc(samp_made[j], 1)

        def column_half(c):
            return slice(c * BANK, (c + 1) * BANK)

        def turn_bank(q):
            return 4 if q == PAIRS - 1 else 2

        def hold(eng, semaphore, value):
            eng.wait_ge(semaphore, value)
            eng.sem_inc(held, 1)

        def load_control(eng, regs):
            eng.load(regs, ctl[0:1, 0:4])
            eng.sem_inc(ctl_read, 1)

        def control_registers(eng, tag):
            return [eng.alloc_register(f"{tag}_{n}") for n in ("layer", "op", "attn", "ffn")]

        def counters(eng, tag):
            regs = [eng.alloc_register(f"{tag}_{n}") for n in ("steps", "attns", "ffns")]
            for r in regs:
                eng.reg_mov(r, 0)
            return regs

        @block.sync
        def _(sp):
            for half in range(HALVES):
                sp.dma_start(xq[:, half * HW:(half + 1) * HW], x[half]).then_inc(x_in, 16)
            sp.dma_start(offw[:, :], offset_w).then_inc(offw_in, 16)
            sp.dma_start(cst[:, :], const).then_inc(const_in, 16)
            sp.dma_start(convw[:, :], conv_w).then_inc(convw_in, 16)
            sp.dma_start(ssmw[:, :], ssm_w).then_inc(ssmw_in, 16)
            sp.dma_start(spread[:, :], spread_w).then_inc(spread_in, 16)
            sp.dma_start(mask8[:, :], masks).then_inc(ctl_in, 16)
            sp.dma_start(stepno[:, :], steps).then_inc(ctl_in, 16)

            for p, groups in ((0, (0, 1)), (1, (0, 1)), (2, (0, 1)), (0, (2,)), (1, (2,)), (2, (2,)),
                              (0, (3,)), (1, (3,)), (2, (3,))):
                sp.wait_ge(part_ready[p], 2)
                for g in groups:
                    sp.dma_start(stack[32 * p:32 * p + 32, g * SEQ:(g + 1) * SEQ],
                                 pieces[p][32 * g:32 * g + 32, :]).then_inc(stack_in[g], 16)

            regs = control_registers(sp, "sp")
            steps_done, _, _ = counters(sp, "sp")
            layer, op = regs[0], regs[1]
            sp.wait_ge(ctl_ready, 1)
            load_control(sp, regs)
            with sp.While(lambda: sp.snap(layer) < LAYERS):
                sp.reg_add(steps_done, steps_done, 1)
                at = sp.snap(sp.snap(layer) * OPS + sp.snap(op), min_val=0, max_val=LAYERS * OPS - 1)
                sp.dma_start(wup, w_up[bass.ds(at, 1), :, :].rearrange("o c n -> (o c) n").unsqueeze(0)
                             .broadcast_to([PAIRS, C, HID + 1])).then_inc(w_up_in, 16)
                sp.dma_start(wdn, w_down[bass.ds(at, 1), :, :].rearrange("o c n -> (o c) n")).then_inc(w_down_in, 16)
                hold(sp, w_up_in, sp.snap(steps_done) * 16)
                hold(sp, w_down_in, sp.snap(steps_done) * 16)
                hold(sp, ctl_ready, sp.snap(steps_done) + 1)
                load_control(sp, regs)

            hold(sp, fin_ready, sp.snap(steps_done) + 1)
            for half in range(HALVES):
                sp.dma_start(out[half], fin[:, half * HW:(half + 1) * HW]).then_inc(out_stored, 16)
            sp.wait_ge(out_stored, 16 * HALVES)

        @block.gpsimd
        def _(pool_e):
            pool_e.memset(ones[:, :], 1.0).then_inc(table_input, 1)
            pool_e.memset(eps[:, :], GN_EPS).then_inc(eps_set, 1)
            pool_e.memset(zero_bf[:, :], 0.0).then_inc(zero_set, 1)
            pool_e.memset(xpad, 0.0).then_inc(pad_zeroed, 1)
            pool_e.memset(wbd[:, :, :], 0.0).then_inc(wbd_zeroed, 1)
            pool_e.sem_inc(chunk_summed, 3)
            pool_e.wait_ge(spread_in, 16)
            pool_e.tensor_copy(picks[:, :].rearrange("p (j b d) -> p b j d", j=PER, b=HALVES),
                               spread[:, :].rearrange("p (b j) -> p b j", b=HALVES).unsqueeze(3)
                               .broadcast_to([96, HALVES, PER, DI])).then_inc(picks_ready, 1)

            with pool_e.Fori(0, ROWS) as kk:
                for half in range(HALVES):
                    it = HALVES * kk + half
                    sampling_chunk(pool_e, it, 2)
                    pool_e.wait_ge(z_ready, 8)
                    for j in range(3):
                        k = 3 * kk + j
                        pool_e.wait_ge(chunk_summed, 3 * it + j + 1)
                        pool_e.tensor_copy(zk[j], zs[:, half, :, :, bass.ds(k * C, C)]).then_inc(zk_ready, 1)

            pool_e.wait_ge(conv_done, 1)
            for t in range(GROUPS):
                pool_e.memset(dA[t], 0.0).then_inc(da_zeroed, 1)
            for t in range(2 * GROUPS):
                pool_e.memset(prod[t], 0.0).then_inc(prod_zeroed, 1)
            for t in range(2):
                pool_e.memset(pick[t], 0.0).then_inc(prod_zeroed, 1)
            pool_e.wait_ge(prod_zeroed, 2 * GROUPS + 2)
            pool_e.sem_inc(prod_ready, GROUPS)
            pool_e.sem_inc(pick_ready, 1)
            pool_e.wait_ge(c_ready, 1)

            def products(it, jp, groups):
                pool_e.wait_ge(prod_summed, 2 * it + jp + 1)
                for g in range(groups):
                    e = 8 * it + GROUPS * jp + g
                    pool_e.wait_ge(scanned, e + GROUPS + 1)
                    pool_e.tensor_tensor(prod[GROUPS * jp + g], state[g], cn, ALU.mult).then_inc(prod_ready, 1)

            with pool_e.Fori(0, PER // 2 - 1) as it:
                for jp in range(2):
                    products(it, jp, GROUPS)
            products(PER // 2 - 1, 0, GROUPS)
            products(PER // 2 - 1, 1, GROUPS - 2)
            pool_e.wait_ge(scanned, DI + GROUPS - 1)
            for c in range(2):
                pool_e.tensor_tensor(prod[-2][:, column_half(c)], state[-2][:, column_half(c)], cn[:, column_half(c)],
                                     ALU.mult).then_inc(late_prod_ready, 1)

        @block.scalar
        def _(act):

            def bring_in(function, n):
                act.activation(unused[:, 0:1], ones[:, :], function).then_inc(act_step, 1)
                act.wait_ge(act_step, n)

            act.wait_ge(table_input, 1)
            bring_in(ACT.Sqrt, 1)
            act.wait_ge(eps_set, 1)
            act.wait_ge(gn_var, 2)
            act.activation(gsd[:, :], mv[:, :, 1], ACT.Sqrt, bias=eps[:, :]).then_inc(gn_sd, 1)

            act.sem_inc(turned_ready, 3)

            def evacuate_filters(n):
                half, side = divmod(n, 2)
                for two in range(2):
                    act.wait_ge(z_done, 2 * n + two + 1)
                    act.activation(zs[:, half, 2 * two:2 * two + 2, side, :], bank(3 + 2 * two, 2)
                                   .rearrange("p (q k) -> p q k", q=2)[:, :, 0:TAPS * C], ACT.Copy).then_inc(z_ready, 1)

            def hats(i):
                act.wait_ge(hat_abs, i + 1)
                v = hat[:, bass.ds(i, 1), :, :, :].rearrange("p i c o y -> p (i c o y)")
                act.activation(v, v, ACT.Relu, bias=1.0, scale=-1.0).then_inc(hat_ready, 1)

            evacuate_filters(0)
            evacuate_filters(1)
            hats(0)
            evacuate_filters(2)
            hats(1)
            evacuate_filters(3)

            with act.Fori(0, ROWS) as kk:
                for half in range(HALVES):
                    it = HALVES * kk + half
                    for j in range(3):
                        act.wait_ge(chunk_summed, 3 * it + j + 1)
                        for side in range(2):
                            s = 2 * j + side
                            act.wait_ge(samp_turned, 6 * it + s + 7)
                            act.activation(sampT[j][:, 2 * side:2 * side + 2].rearrange("p q h n -> p (q h n)"),
                                           bank(2 + 2 * (s % 3), 2), ACT.Copy).then_inc(turned_ready, 1)
                        if j == 1:
                            hats(it + HALVES)


            def layer_norm(n):
                act.wait_ge(ln_cen, n + 1)
                act.activation(sq[:, :], bank(1), ACT.Square).then_inc(ln_sq, 1)
                act.wait_ge(ln_var, n + 1)
                act.activation(root[:, :], bank(2)[:, 0:16], ACT.Sqrt, bias=eps[:, :]).then_inc(ln_sd, 1)

            layer_norm(0)
            act.wait_ge(xs_done, 1)
            act.activation(xs, bank(4, 2), ACT.Copy).then_inc(xs_ready, 1)
            bring_in(ACT.Exp, 2)
            for c in range(2):
                act.wait_ge(delta_done, c + 1)
                act.activation(pieces[0][:, column_half(c)], bank(2 + c), ACT.Copy).then_inc(part_ready[0], 1)
            for c in range(2):
                act.wait_ge(part_rest, c + 1)
                act.activation(pieces[1][:, column_half(c)], rest[:, column_half(c)], ACT.Copy)\
                   .then_inc(part_ready[1], 1)
            act.wait_ge(c_done, 2)
            act.activation(cn, bank(4, 2), ACT.Copy).then_inc(c_ready, 1)

            act.wait_ge(da_zeroed, GROUPS)
            act.sem_inc(da_ready, 2)

            def inner_tail(ap):
                return ap.rearrange("p (q n) -> p q n", q=PAIRS)[:, :, 1:HW]

            act.wait_ge(const_in, 16)
            onehot = part["onehot"].rearrange("p (b w) -> p b w", b=HALVES)
            with act.Fori(0, PER // 2) as it:
                for jp in range(2):
                    j = 2 * it + jp
                    for g in range(GROUPS):
                        e = 8 * it + GROUPS * jp + g
                        act.wait_ge(delta_spread, e + 1)
                        act.wait_ge(scanned, e + 1)
                        act.activation(inner_tail(dA[g]), inner_tail(bank(2 + 2 * (g % 2), 2)), ACT.Exp,
                                       scale=wt["a"][:, bass.ds(PER * g + j, 1)]).then_inc(da_ready, 1)
                    act.wait_ge(prod_summed, j + 1)
                    act.activation(pick[jp].rearrange("p (b w) -> p b w", b=HALVES),
                                   onehot[:, :, bass.ds(PER - 1 - j, PER)], ACT.Copy).then_inc(pick_ready, 1)

            act.wait_ge(gate_in_done, 1)
            act.activation(gate, bank(6, 2), ACT.Silu).then_inc(gate_ready, 1)
            bring_in(ACT.Sqrt, 3)
            layer_norm(1)

            regs = control_registers(act, "act")
            steps_done, attns, ffns = counters(act, "act")
            act.wait_ge(ctl_ready, 1)
            load_control(act, regs)
            with act.While(lambda: act.snap(regs[0]) < LAYERS):
                act.reg_add(steps_done, steps_done, 1)
                with act.If(act.snap(regs[2]) > 0):
                    a = act.snap(attns)
                    at = act.snap(act.snap(regs[0]) * OPS + act.snap(regs[1]), min_val=0, max_val=LAYERS * OPS - 1)
                    act.dma_start(wat, w_attn[bass.ds(at, 1), :, :].rearrange("o c n -> (o c) n").unsqueeze(0)
                                  .broadcast_to([PAIRS, C, 128])).then_inc(w_attn_in, 16)
                    act.activation(unused[:, 1:2], ones[:, :], ACT.Exp).then_inc(exp_table, 1)
                    act.wait_ge(exp_table, a + 1)
                    act.wait_ge(qkv_done, 3 * a + 1)
                    act.activation(qs, bank(0), ACT.Copy).then_inc(qv_ready, 1)
                    act.wait_ge(qkv_done, 3 * a + 3)
                    act.activation(vs, bank(2), ACT.Copy).then_inc(qv_ready, 1)
                    for q in range(PAIRS):
                        act.wait_ge(max_ready, PAIRS * a + q + 1)
                        if q >= 2:
                            act.wait_ge(probT_done, PAIRS * a + q - 1)
                        for c in range(4):
                            i = 4 * q + c
                            act.activation(es[q % 2][:, c, :], bank(4 + 2 * (q % 2), 2)[:, c * HW:(c + 1) * HW],
                                           ACT.Exp, bias=nm[:, i:i + 1], scale=SCALE,
                                           accum_out=sm[:, i:i + 1]).then_inc(exp_done, 1)
                    act.wait_ge(ri_turn_done, a + 1)
                    act.activation(ri_turned, bank(1), ACT.Copy).then_inc(ri_turned_ready, 1)
                    act.reg_add(attns, attns, 1)
                with act.If(act.snap(regs[3]) > 0):
                    f = act.snap(ffns)
                    act.activation(unused[:, 2:3], ones[:, :], ACT.Relu).then_inc(relu_table, 1)
                    act.wait_ge(relu_table, f + 1)
                    act.wait_ge(w_down_in, act.snap(steps_done) * 16)
                    for q in range(2):
                        act.wait_ge(up_done, PAIRS * f + q + 1)
                        act.activation(hid[:, q, :], bank(4 + q), ACT.Relu, bias=wdn[:, C:C + 1]).then_inc(act_relu, 1)
                    act.reg_add(ffns, ffns, 1)
                hold(act, ctl_ready, act.snap(steps_done) + 1)
                load_control(act, regs)

        @block.vector
        def _(dve):
            made = [0]

            def step(ins):
                ins.then_inc(dve_step, 1)
                made[0] += 1

            def settle():
                dve.wait_ge(dve_step, made[0])

            dve.wait_ge(x_in, 16 * HALVES)
            for half in range(HALVES):
                step(dve.bn_stats(stats[:, half, :], xq[:, half * HW:(half + 1) * HW]))
            settle()
            for half in range(HALVES):
                dve.bn_aggr(mv[:, half, :], stats[:, half, :]).then_inc(gn_var, 1)
            dve.wait_ge(gn_sd, 1)
            step(dve.reciprocal(grs[:, :], gsd[:, :]))
            settle()
            dve.wait_ge(gn_var, 2)
            dve.wait_ge(pad_zeroed, 1)
            for half in range(HALVES):
                dve.tensor_scalar(xpad[:, half, 1:1 + SIDE, 1:1 + SIDE],
                                  xq[:, half * HW:(half + 1) * HW].rearrange("p (y x) -> p y x", y=SIDE),
                                  mv[:, half, 0:1], grs[:, half:half + 1], ALU.subtract, ALU.mult)\
                   .then_inc(xn_ready, 1)
            dve.wait_ge(xn_ready, HALVES)
            dve.tensor_copy(xn.rearrange("p (b y x) -> p b y x", b=HALVES, y=SIDE),
                            xpad[:, :, 1:1 + SIDE, 1:1 + SIDE]).then_inc(xn_ready, 1)

            dve.wait_ge(off_done, 1)
            dve.wait_ge(const_in, 16)
            dve.scalar_tensor_tensor(off, bank(2), part["offset_b"], part["grid"], ALU.add, ALU.add)\
               .then_inc(off_ready, 1)
            def distances(half, kk):
                i = HALVES * kk + half
                pos = bank(1)[:, half * HW:(half + 1) * HW].rearrange("p (c o) -> p c o", c=8)[:, :, bass.ds(6 * kk, 6)]
                v = hat[:, bass.ds(i, 1), :, :, :].rearrange("p i c o y -> p (i c) o y")
                dve.tensor_tensor(v, pos.unsqueeze(3).broadcast_to([128, 8, 6, SIDE]),
                                  part["level"].unsqueeze(1).unsqueeze(1).broadcast_to([128, 8, 6, SIDE]),
                                  ALU.subtract).then_inc(hat_diff, 1)
                dve.wait_ge(hat_diff, i + 1)
                flat = v.rearrange("p c o y -> p (c o y)")
                dve.scalar_tensor_tensor(flat, flat, -1.0, flat, ALU.mult, ALU.max).then_inc(hat_abs, 1)

            dve.wait_ge(offT_done, 1)
            for half in range(HALVES):
                distances(half, 0)
            with dve.Fori(0, ROWS) as kk:
                for half in range(HALVES):
                    for j in range(2):
                        sampling_chunk(dve, HALVES * kk + half, j)
                    distances(half, kk + 1)

            dve.wait_ge(conv_done, 1)
            dve.tensor_scalar(t1[:, :], bank(0), part["conv_b"], None, ALU.add).then_inc(ln_in, 1)

            def layer_norm(n, dst):
                dve.wait_ge(ln_sq, n + 1)
                step(dve.tensor_copy(cen[:, :], bank(1)))
                dve.wait_ge(ln_sd, n + 1)
                step(dve.reciprocal(inv[:, :], root[:, :]))
                settle()
                dve.tensor_copy(inv_wide[:, :].rearrange("p (k c) -> p k c", k=16),
                                inv[:, :].unsqueeze(2).broadcast_to([128, 16, C])).then_inc(ln_inv, 1)
                dve.wait_ge(ln_turned, n + 1)
                return dve.tensor_tensor(dst[:, :], cen[:, :], bank(2), ALU.mult)

            layer_norm(0, tn).then_inc(ln_out, 1)

            dve.wait_ge(ctl_in, 32)
            tabv = tab[:, :].rearrange("p (o s l) -> p o s l", o=OPS, s=3)
            m8 = mask8[:, :].rearrange("p (s o l) -> p s o l", s=2, o=OPS)
            left = stepno[:, LAYERS:2 * LAYERS].unsqueeze(1).broadcast_to([1, OPS, LAYERS])
            for s in range(2):
                step(dve.tensor_tensor(tabv[:, :, 1 + s, :], m8[:, s, :, :], left, ALU.mult))
            settle()
            step(dve.tensor_tensor(tabv[:, :, 0, :], tabv[:, :, 1, :], tabv[:, :, 2, :], ALU.max))
            step(dve.memset(cur[:, :], -1.0))

            for c in range(2):
                dve.wait_ge(part_ready[0], c + 1)
                dve.tensor_tensor(rest[:, column_half(c)], bank(2 + c), pieces[0][:, column_half(c)], ALU.subtract)\
                   .then_inc(part_rest, 1)
            dve.wait_ge(part_rest, 2)
            for c in range(2):
                dve.wait_ge(part_ready[1], c + 1)
                dve.tensor_tensor(pieces[2][:, column_half(c)], rest[:, column_half(c)], pieces[1][:, column_half(c)],
                                  ALU.subtract).then_inc(part_ready[2], 1)
            dve.wait_ge(xs_ready, 1)
            dve.wait_ge(b_done, 2)
            dve.tensor_tensor(bx, xs, bank(0, 2), ALU.mult).then_inc(bx_ready, 1)

            dve.wait_ge(bx_ready, 1)
            dve.sem_inc(dbx_ready, 2)
            dve.sem_inc(scanned, GROUPS)

            def added(it, i):
                e = 8 * it + i
                dve.wait_ge(da_ready, e + 3)
                dve.wait_ge(scanned, e + 1)
                dve.tensor_tensor(dbx[i % GROUPS], bx, bank(2 + 2 * (i % 2), 2), ALU.mult).then_inc(dbx_ready, 1)

            def scan(it, i):
                e = 8 * it + i
                dve.wait_ge(dbx_ready, e + 3)
                dve.wait_ge(prod_ready, e + 1)
                dve.tensor_tensor_scan(state[i % GROUPS], dA[i % GROUPS], dbx[i % GROUPS], 0.0, ALU.mult, ALU.add)\
                   .then_inc(scanned, 1)

            def turn_but_last_scan(it):
                added(it, 0)
                for i in range(1, 2 * GROUPS):
                    added(it, i)
                    scan(it, i - 1)

            with dve.Fori(0, PER // 2 - 1) as it:
                turn_but_last_scan(it)
                scan(it, 2 * GROUPS - 1)
            turn_but_last_scan(PER // 2 - 1)
            dve.wait_ge(dbx_ready, DI + 2)
            dve.wait_ge(prod_ready, DI)
            for c in range(2):
                dve.tensor_tensor_scan(state[-1][:, column_half(c)], dA[-1][:, column_half(c)],
                                       dbx[-1][:, column_half(c)], 0.0, ALU.mult, ALU.add).then_inc(late_scanned, 1)
                dve.wait_ge(late_scanned, c + 1)
                dve.tensor_tensor(prod[-1][:, column_half(c)], state[-1][:, column_half(c)], cn[:, column_half(c)],
                                  ALU.mult).then_inc(last_prod_ready, 1)
            dve.wait_ge(gate_ready, 1)
            for c in range(2):
                dve.wait_ge(y_done, c + 1)
                dve.tensor_tensor(gated[:, column_half(c)], bank(c), gate[:, column_half(c)], ALU.mult)\
                   .then_inc(gated_ready, 1)
            dve.wait_ge(mix_done, 1)
            for half in range(HALVES):
                ins = dve.tensor_tensor(t2[:, half * HW:(half + 1) * HW], t1[:, half * HW:(half + 1) * HW],
                                        bank(2)[:, half * HW:(half + 1) * HW], ALU.add)
                if half:
                    ins.then_inc(ln_in, 1)
                else:
                    step(ins)
            settle()
            layer_norm(1, h).then_inc(h_ready, 1)

            regs = control_registers(dve, "dve")
            steps_done, attns, ffns = counters(dve, "dve")
            op_reg = dve.alloc_register("dve_chosen")

            def next_step(n):
                hold(dve, row_done, n + 1)
                c = 6 * n
                row = bank(3)[0:1, 0:OPS]
                dve.max(top[:, :], row).then_inc(ctl_step, 1)
                hold(dve, ctl_step, c + 1)
                dve.max_index(idx[:, :], top[:, :], row).then_inc(ctl_step, 1)
                hold(dve, ctl_step, c + 2)
                dve.load([op_reg], idx[0:1, 0:1])
                op = dve.snap(op_reg, min_val=0, max_val=OPS - 1)
                v = cand[:, :].rearrange("p (s l) -> p s l", s=3)
                dve.scalar_tensor_tensor(v, stepno[:, 0:LAYERS].unsqueeze(1).broadcast_to([1, 3, LAYERS]), cur[:, 0:1],
                                         tab[:, bass.ds(op * (3 * LAYERS), 3 * LAYERS)]
                                         .rearrange("p (s l) -> p s l", s=3), ALU.is_gt, ALU.mult).then_inc(ctl_step, 1)
                dve.wait_ge(ctl_step, c + 3)
                dve.tensor_reduce(best[:, 0:3], v, AX.X, ALU.max).then_inc(ctl_step, 1)
                dve.wait_ge(ctl_step, c + 4)
                dve.tensor_scalar(cur[:, :], best[:, 0:1], -1.0, float(LAYERS), ALU.mult, ALU.add).then_inc(ctl_step, 1)
                dve.wait_ge(ctl_read, 3 * n + 1)
                dve.tensor_scalar(ctl[:, 2:4], best[:, 1:3], best[:, 0:1], None, ALU.is_equal).then_inc(ctl_step, 1)

            def publish(n, attns_done, ffns_done):
                dve.tensor_copy(ctl[:, 1:2], idx[:, 0:1]).then_inc(ctl_words, 1)
                dve.wait_ge(ctl_step, 6 * n + 5)
                dve.tensor_copy(ctl[:, 0:1], cur[:, :]).then_inc(ctl_words, 1)
                dve.wait_ge(ctl_words, 2 * n + 2)
                dve.wait_ge(ctl_step, 6 * n + 6)
                dve.sem_inc(ctl_ready, 1)
                dve.load(regs, ctl[0:1, 0:4])
                hold(dve, h_ready, 1 + attns_done + ffns_done)
                dve.tensor_tensor(fin[:, :], t2[:, :], h[:, :], ALU.add).then_inc(fin_ready, 1)

            dve.sem_inc(ctl_read, 1)
            next_step(0)
            publish(0, 0, 0)
            with dve.While(lambda: dve.snap(regs[0]) < LAYERS):
                dve.reg_add(steps_done, steps_done, 1)
                with dve.If(dve.snap(regs[2]) > 0):
                    a = dve.snap(attns)
                    dve.wait_ge(w_attn_in, 16 * a + 16)
                    dve.wait_ge(wbd_zeroed, 1)
                    for q in range(PAIRS):
                        s = slice(C * q, C * q + C)
                        dve.tensor_copy(wbd[s, :, s], wat[s, :].rearrange("p (w n) -> p w n", w=4))\
                           .then_inc(bd_ready, 1)
                    dve.wait_ge(qkv_done, 3 * a + 2)
                    dve.tensor_copy(ks, bank(1)).then_inc(k_ready, 1)

                    chain = [0]

                    def attention_step(ins):
                        ins.then_inc(attn_step, 1)
                        chain[0] += 1
                        dve.wait_ge(attn_step, 5 * a + chain[0])

                    def maxima(q):
                        dve.wait_ge(score_done, PAIRS * a + q + 1)
                        m = slice(4 * q, 4 * q + 4)
                        attention_step(dve.tensor_reduce(mx[:, m], bank(4 + 2 * (q % 2), 2)
                                                         .rearrange("p (c k) -> p c k", c=4), AX.X, ALU.max))
                        dve.tensor_scalar(nm[:, m], mx[:, m], -SCALE, None, ALU.mult).then_inc(max_ready, 1)

                    def turned(q):
                        dve.wait_ge(probT_done, PAIRS * a + q + 1)
                        dve.tensor_copy(pt[q % 2], bank(turn_bank(q), 2)).then_inc(probT_ready, 1)

                    maxima(0)
                    maxima(1)
                    for q in range(PAIRS - 1):
                        turned(q)
                        if q + 2 < PAIRS:
                            maxima(q + 2)
                    dve.wait_ge(exp_done, 16 * a + 16)
                    attention_step(dve.reciprocal(ri, sm))
                    dve.tensor_copy(ri_wide.rearrange("p (c q d) -> p c q d", c=4, q=PAIRS),
                                    ri.rearrange("p (q c) -> p c q", q=PAIRS).unsqueeze(3)
                                    .broadcast_to([128, 4, PAIRS, C])).then_inc(ri_wide_ready, 1)
                    turned(PAIRS - 1)
                    dve.wait_ge(ri_turned_ready, a + 1)
                    dve.wait_ge(pv_done, a + 1)
                    dve.tensor_tensor(ot, bank(0), ri_turned, ALU.mult).then_inc(head_ready, 1)
                    dve.wait_ge(attn_out, a + 1)
                    dve.tensor_copy(h[:, :], bank(1)).then_inc(h_ready, 1)
                    dve.reg_add(attns, attns, 1)
                with dve.If(dve.snap(regs[3]) > 0):
                    f = dve.snap(ffns)
                    dve.wait_ge(w_up_in, dve.snap(steps_done) * 16)
                    dve.wait_ge(w_down_in, dve.snap(steps_done) * 16)
                    for q in range(2, PAIRS):
                        dve.wait_ge(up_done, PAIRS * f + q + 1)
                        dve.tensor_scalar(hid[:, q, :], bank(4 + q), wdn[:, C:C + 1], 0.0, ALU.add, ALU.max)\
                           .then_inc(dve_relu, 1)
                    dve.wait_ge(down_done, f + 1)
                    dve.tensor_scalar(h[:, :], bank(0), wup[:, HID:HID + 1], None, ALU.add).then_inc(h_ready, 1)
                    dve.reg_add(ffns, ffns, 1)
                k = dve.snap(steps_done)
                next_step(k)
                dve.wait_ge(fin_ready, k)
                publish(k, dve.snap(attns), dve.snap(ffns))

        @block.tensor
        def _(pe):
            def quad(q):
                return slice(C * q, C * q + C)

            def offset_taps(taps):
                for t in taps:
                    dy, dx = divmod(t, 3)
                    ins = pe.matmul(bank(2), offw[:, t * 128:(t + 1) * 128], xpad[:, :, dy:dy + SIDE, dx:dx + SIDE],
                                    start=t == 0, stop=t == TAPS - 1)
                return ins

            def filters(n):
                half, side = divmod(n, 2)
                for q in range(PAIRS):
                    if n > 1 and q == 0:
                        keep_warm(4)
                    if n and q % 2 == 0:
                        pe.wait_ge(z_ready, 2 * n - 1 + q // 2)
                    px = xn[quad(q), half * HW + side * 128:half * HW + side * 128 + 128]
                    ins = pe.matmul(bank(3 + q)[:, 0:TAPS * C], px, convw[quad(q), :], start=True, stop=True)
                    if q % 2:
                        ins.then_inc(z_done, 1)

            def keep_warm(n, at=7):
                for _ in range(n):
                    pe.matmul(bank(at), zero_bf[:, 0:128], zero_bf[:, :], start=True, stop=True)

            pe.sem_inc(samp_turned, 6)
            pe.wait_ge(zero_set, 1)
            keep_warm(12)
            pe.wait_ge(offw_in, 16)
            pe.wait_ge(xn_ready, HALVES)
            offset_taps(range(TAPS)).then_inc(off_done, 1)
            pe.wait_ge(convw_in, 16)
            pe.wait_ge(xn_ready, HALVES + 1)
            filters(0)
            pe.wait_ge(const_in, 16)
            pe.wait_ge(off_ready, 1)
            for c in range(4):
                ins = pe.transpose(bank(1)[:, c * 128:(c + 1) * 128], off[:, c * 128:(c + 1) * 128], ident)
            ins.then_inc(offT_done, 1)
            for n in range(1, 4):
                filters(n)

            pe.wait_ge(x_in, 16 * HALVES)
            pe.matmul(bank(0), ident, xq[:, :], start=True, stop=False)
            pe.wait_ge(z_ready, 8)

            def turn(it, j):
                pe.wait_ge(samp_made[j], it + 1)
                for side in range(2):
                    s = 2 * j + side
                    pe.wait_ge(turned_ready, 6 * it + s + 1)
                    for q in range(2):
                        for hh in range(2):
                            for t in range(2):
                                at = q * BANK + hh * HW + t * 128
                                ins = pe.transpose(bank(2 + 2 * (s % 3), 2)[:, at:at + 128],
                                                   samp[j][:, 4 * t + 2 * side + q, hh * 128:hh * 128 + 128], ident)
                    ins.then_inc(samp_turned, 1)

            def tap_sum(it, half, j):
                pe.wait_ge(zk_ready, 3 * it + j + 1)
                pe.wait_ge(turned_ready, 6 * it + 2 * j + 2 + 3)
                for hh in range(2):
                    for q in range(PAIRS):
                        ins = pe.matmul(bank(0)[quad(q), half * HW:(half + 1) * HW], zk[j][:, q, hh, :],
                                        sampT[j][:, q, hh, :], start=False, stop=False)
                ins.then_inc(chunk_summed, 1)

            with pe.Fori(0, ROWS) as kk:
                chunks = [(HALVES * kk + half, half, j) for half in range(HALVES) for j in range(3)]
                for n, (it, half, j) in enumerate(chunks):
                    turn(it, j)
                    if n:
                        tap_sum(*chunks[n - 1])
                tap_sum(*chunks[-1])
            pe.matmul(bank(0), zero_bf[:, 0:128], zero_bf[:, :], start=False, stop=True).then_inc(conv_done, 1)

            def layer_norm(n, src):
                pe.wait_ge(ln_in, n + 1)
                pe.matmul(bank(1), part["centre"], src[:, :], start=True, stop=True).then_inc(ln_cen, 1)
                keep_warm(4)
                pe.wait_ge(ln_sq, n + 1)
                for c in range(4):
                    ins = pe.matmul(bank(2)[:, PAIRS * c:PAIRS * (c + 1)], sq[:, c * 128:(c + 1) * 128], part["pairs"],
                                    start=True, stop=True)
                ins.then_inc(ln_var, 1)
                keep_warm(4)
                pe.wait_ge(ln_inv, n + 1)
                for c in range(4):
                    ins = pe.transpose(bank(2)[:, c * 128:(c + 1) * 128], inv_wide[:, c * 128:(c + 1) * 128], ident)
                ins.then_inc(ln_turned, 1)

            layer_norm(0, t1)

            def project(at, weights, inc):
                for c in range(2):
                    pe.matmul(bank(at + c), weights, xs[:, column_half(c)], start=True, stop=True).then_inc(inc, 1)

            pe.wait_ge(ssmw_in, 16)
            pe.wait_ge(ln_out, 1)
            for q in range(PAIRS):
                for half in range(HALVES):
                    ins = pe.matmul(bank(4, 2)[DI * half:DI * half + DI, q * HW:(q + 1) * HW],
                                    wt["w_xs"][:, q * DI:(q + 1) * DI], tn[:, half * HW:(half + 1) * HW],
                                    start=True, stop=True)
            ins.then_inc(xs_done, 1)

            def gate_input(q):
                for half in range(HALVES):
                    at = (HALVES * q + half) * 128
                    ins = pe.matmul(bank(6, 2)[:, q * HW:(q + 1) * HW], wt["w_gate"][:, at:at + 128],
                                    tn[:, half * HW:(half + 1) * HW], start=half == 0, stop=half == 1)
                return ins

            gate_input(0)
            pe.wait_ge(xs_ready, 1)
            project(2, wt["w_delta"], delta_done)
            project(0, wt["w_b"], b_done)
            project(4, wt["w_c"], c_done)
            for q in range(1, PAIRS):
                ins = gate_input(q)
            ins.then_inc(gate_in_done, 1)

            pe.wait_ge(picks_ready, 1)
            pe.wait_ge(bx_ready, 1)
            for c in range(2):
                pe.matmul(bank(c), zero_bf[:, 0:128], zero_bf[:, :], start=True, stop=False)
            pe.wait_ge(c_ready, 1)
            pe.wait_ge(prod_ready, GROUPS)
            pe.wait_ge(pick_ready, 1)

            def add_products(jp, c, stop=False):
                for g in range(GROUPS):
                    ins = pe.matmul(bank(c)[quad(g), :], pick[jp], prod[GROUPS * jp + g][:, column_half(c)],
                                    start=False, stop=stop)
                return ins

            with pe.Fori(0, PER // 2) as it:
                for jp in range(2):
                    j = 2 * it + jp
                    for g in range(GROUPS):
                        e = 8 * it + GROUPS * jp + g
                        pe.wait_ge(stack_in[g], 16 * 3)
                        pe.wait_ge(da_ready, e + 1)
                        pe.wait_ge(dbx_ready, e + 1)
                        for c in range(2):
                            ins = pe.matmul(bank(2 + 2 * (g % 2) + c), picks[:, bass.ds(j * 128, 128)],
                                            stack[0:96, g * SEQ + c * BANK:g * SEQ + (c + 1) * BANK],
                                            start=True, stop=True)
                        ins.then_inc(delta_spread, 1)
                        if g == 0:
                            add_products(jp, 1).then_inc(prod_summed, 1)
                    pe.wait_ge(prod_ready, GROUPS * j + GROUPS)
                    pe.wait_ge(pick_ready, j + 1)
                    add_products(1 - jp, 0)
            add_products(0, 1)
            pe.wait_ge(dbx_ready, DI + 2)
            keep_warm(4, 2)
            pe.wait_ge(prod_ready, DI + GROUPS - 2)
            pe.wait_ge(pick_ready, PER + 1)
            for c in range(2):
                pe.wait_ge(late_prod_ready, c + 1)
                pe.wait_ge(last_prod_ready, c + 1)
                add_products(1, c, True).then_inc(y_done, 1)

            for q in range(PAIRS):
                pe.wait_ge(gated_ready, q // 2 + 1)
                for half in range(HALVES):
                    ins = pe.matmul(bank(2)[quad(q), half * HW:(half + 1) * HW],
                                    wt["w_out"][:, half * C:(half + 1) * C],
                                    gated[:, q * HW:(q + 1) * HW], start=True, stop=True)
            ins.then_inc(mix_done, 1)
            layer_norm(1, t2)

            regs = control_registers(pe, "pe")
            steps_done, attns, ffns = counters(pe, "pe")

            def first_token(n):
                pe.wait_ge(h_ready, n)
                pe.matmul(bank(3)[0:1, 0:32], h[:, 0:1], ident[:, 0:C], start=True, stop=True).then_inc(row_done, 1)

            first_token(1)
            keep_warm(14)
            pe.wait_ge(ctl_ready, 1)
            load_control(pe, regs)
            with pe.While(lambda: pe.snap(regs[0]) < LAYERS):
                pe.reg_add(steps_done, steps_done, 1)
                keep_warm(10)
                with pe.If(pe.snap(regs[2]) > 0):
                    a = pe.snap(attns)
                    keep_warm(9)
                    pe.wait_ge(bd_ready, PAIRS * a + PAIRS)
                    for w in range(2):
                        pe.matmul(bank(w), wbd[:, w, :], h[:, :], start=True, stop=True).then_inc(qkv_done, 1)
                    for c in range(4):
                        ins = pe.matmul(bank(2)[:, c * 128:(c + 1) * 128], h[:, c * 128:(c + 1) * 128], wbd[:, 2, :],
                                        start=True, stop=True)
                    ins.then_inc(qkv_done, 1)
                    pe.wait_ge(qv_ready, 2 * a + 1)
                    pe.wait_ge(k_ready, a + 1)

                    def scores(q):
                        if q >= 2:
                            pe.wait_ge(exp_done, 16 * a + 4 * q - 4)
                        for half in range(HALVES):
                            for t in range(2):
                                c0 = half * HW + t * 128
                                ins = pe.matmul(bank(4 + 2 * (q % 2) + half)[:, t * HW:(t + 1) * HW],
                                                qs[quad(q), c0:c0 + 128], ks[quad(q), half * HW:(half + 1) * HW],
                                                start=True, stop=True)
                        ins.then_inc(score_done, 1)

                    def turn_probabilities(q):
                        pe.wait_ge(exp_done, 16 * a + 4 * q + 4)
                        if 0 < q < PAIRS - 1:
                            pe.wait_ge(probT_ready, PAIRS * a + q)
                        for half in range(HALVES):
                            for kt in range(2):
                                for t in range(2):
                                    at = ((half * 2 + kt) * 2 + t) * 128
                                    ins = pe.transpose(bank(turn_bank(q), 2)[:, at:at + 128],
                                                       es[q % 2][:, 2 * half + t, kt * 128:kt * 128 + 128], ident)
                        ins.then_inc(probT_done, 1)

                    def values_times_probabilities(q0):
                        pe.wait_ge(probT_ready, PAIRS * a + q0 + 2)
                        for half in range(HALVES):
                            for kt in range(2):
                                for q in (q0, q0 + 1):
                                    v0 = (2 * half + kt) * 128 + C * q
                                    ins = pe.matmul(bank(0)[quad(q), half * HW:(half + 1) * HW], vs[:, v0:v0 + C],
                                                    pt[q % 2][:, (2 * half + kt) * HW:(2 * half + kt + 1) * HW],
                                                    start=kt == 0, stop=kt == 1)
                        return ins

                    scores(0)
                    scores(1)
                    keep_warm(6, 1)
                    for q in range(2):
                        turn_probabilities(q)
                        scores(q + 2)
                    pe.wait_ge(qv_ready, 2 * a + 2)
                    values_times_probabilities(0)
                    turn_probabilities(2)
                    turn_probabilities(3)
                    pe.wait_ge(ri_wide_ready, a + 1)
                    for c in range(4):
                        ins = pe.transpose(bank(1)[:, c * 128:(c + 1) * 128], ri_wide[:, c * 128:(c + 1) * 128], ident)
                    ins.then_inc(ri_turn_done, 1)
                    values_times_probabilities(2).then_inc(pv_done, 1)
                    keep_warm(4)
                    pe.wait_ge(head_ready, a + 1)
                    pe.matmul(bank(1), wbd[:, 3, :], ot, start=True, stop=True).then_inc(attn_out, 1)
                    keep_warm(4)
                    pe.reg_add(attns, attns, 1)
                with pe.If(pe.snap(regs[3]) > 0):
                    f = pe.snap(ffns)
                    pe.wait_ge(w_up_in, pe.snap(steps_done) * 16)
                    pe.wait_ge(h_ready, 1 + pe.snap(attns) + f)
                    for q in range(PAIRS):
                        pe.matmul(bank(4 + q), wup[quad(q), 0:HID], h[quad(q), :], start=True, stop=True)\
                          .then_inc(up_done, 1)
                    pe.wait_ge(w_down_in, pe.snap(steps_done) * 16)
                    for q in range(PAIRS):
                        if q < 2:
                            pe.wait_ge(act_relu, 2 * f + q + 1)
                        else:
                            pe.wait_ge(dve_relu, 2 * f + q - 1)
                        ins = pe.matmul(bank(0)[quad(q), :], wdn[:, 0:C], hid[:, q, :], start=True, stop=True)
                    ins.then_inc(down_done, 1)
                    pe.reg_add(ffns, ffns, 1)
                first_token(1 + pe.snap(attns) + pe.snap(ffns))
                keep_warm(14)
                hold(pe, ctl_ready, pe.snap(steps_done) + 1)
                load_control(pe, regs)


def _constants(np):
    level = np.arange(SIDE, dtype=np.float32)
    grid = np.zeros((PAIRS, C, HALVES, SIDE, SIDE), np.float32)
    for k in range(TAPS):
        kh, kw = divmod(k, 3)
        grid[:, 2 * k] = (level - 1 + kh)[:, None]
        grid[:, 2 * k + 1] = (level - 1 + kw)[None, :]
    centre = np.eye(128, dtype=np.float32) - np.kron(np.eye(PAIRS, dtype=np.float32),
                                                     np.full((C, C), 1.0 / C, np.float32))
    pairs = np.kron(np.eye(PAIRS, dtype=np.float32), np.full((C, 1), 1.0 / C, np.float32))
    onehot = np.zeros((HALVES, DI, HALVES, 2 * PER - 1), np.float32)
    for half in range(HALVES):
        onehot[half, :, half, PER - 1] = 1.0
    return {"pairs": pairs, "onehot": onehot.reshape(128, -1), "level": np.tile(level, (128, 1)),
            "ident": np.eye(128, dtype=np.float32), "centre": centre,
            "grid": grid.reshape(128, TOK)}


def _packed(np, where, width, parts):
    out = np.zeros((128, width), np.float32)
    for name, (a, b) in where.items():
        out[:, a:b] = parts[name]
    return out


def kernel(**inputs):
    import numpy as np
    import concourse.bacc as bacc
    import ml_dtypes
    from concourse.bass_utils import run_bass_kernel_spmd

    g = {k: np.asarray(v) for k, v in inputs.items()}

    def quad_rows(a):
        return np.tile(a, (PAIRS, 1))

    def block_diagonal(a, n):
        out = np.zeros((n, a.shape[0], n, a.shape[1]), a.dtype)
        for i in range(n):
            out[i, :, i] = a
        return out.reshape(n * a.shape[0], n * a.shape[1])

    def group_columns(a):
        bd = block_diagonal(a, HALVES).reshape(128, HALVES, GROUPS, PER)
        return bd.transpose(0, 2, 1, 3).reshape(128, 128)

    parts = _constants(np)
    off_b = np.zeros(C, np.float32)
    off_b[:OFFS] = g["L0_conv_offset_b"]
    parts["offset_b"] = quad_rows(off_b[:, None])
    parts["conv_b"] = quad_rows(g["L0_conv_bias"][:, None])
    ow = np.zeros((TAPS, C, C), np.float32)
    ow[:, :, :OFFS] = g["L0_conv_offset_w"].reshape(OFFS, C, TAPS).transpose(2, 1, 0)
    offset_w = np.concatenate([block_diagonal(w, PAIRS) for w in ow], axis=1)
    conv_w = quad_rows(g["L0_conv_weight"].reshape(C, C, TAPS).transpose(1, 2, 0).reshape(C, TAPS * C))
    w_out = np.zeros((GROUPS, HALVES, PER, HALVES, C), np.float32)
    for half in range(HALVES):
        w_out[:, half, :, half] = g["L1_attn_W_out"].reshape(GROUPS, PER, C)
    w_in = g["L1_attn_W_in"]
    w_gate = np.zeros((C, HALVES, GROUPS, HALVES, PER), np.float32)
    for half in range(HALVES):
        w_gate[:, half, :, half] = w_in[:, DI:].reshape(C, GROUPS, PER)
    ssm = {"w_xs": block_diagonal(w_in[:, :DI], PAIRS), "w_delta": group_columns(g["L1_attn_W_delta"]),
           "w_b": block_diagonal(g["L1_attn_W_B"], HALVES), "w_c": block_diagonal(g["L1_attn_W_C"], HALVES),
           "w_gate": block_diagonal(w_gate.reshape(C, -1), PAIRS),
           "w_out": w_out.reshape(128, HALVES * C), "a": np.tile(g["L1_attn_A"].T, (HALVES, 1))}
    steps = np.concatenate([np.arange(LAYERS), LAYERS - np.arange(LAYERS)]).astype(np.float32)[None]
    masks = np.stack([g["L1_ffn_attn_mask"].T, g["L1_ffn_ffn_mask"].T]).reshape(1, -1)
    n = LAYERS * OPS
    w_attn = np.concatenate([g[f"L1_ffn_{w}"].reshape(n, C, C) for w in ("wq", "wk", "wv", "wo")], axis=2)
    w_up = np.concatenate([g["L1_ffn_ffn_w1"].reshape(n, C, HID), g["L1_ffn_ffn_b2"].reshape(n, C, 1)], axis=2)
    w_down = np.concatenate([g["L1_ffn_ffn_w2"].reshape(n, HID, C), g["L1_ffn_ffn_b1"].reshape(n, HID, 1)], axis=2)
    arrays = {
        "x_dram": g["x"].reshape(B, C, HW),
        "const_dram": _packed(np, CONST, CONST_W, parts),
        "offset_w_dram": offset_w, "conv_w_dram": conv_w,
        "ssm_w_dram": _packed(np, SSM, SSM_W, ssm),
        "spread_dram": np.tile(np.eye(32, dtype=np.float32), (3, 1)).astype(ml_dtypes.bfloat16),
        "masks_dram": masks, "steps_dram": steps,
        "w_attn_dram": w_attn, "w_up_dram": w_up, "w_down_dram": w_down,
    }
    arrays = {k: np.ascontiguousarray(v) for k, v in arrays.items()}
    nc = bacc.Bacc("TRN2", target_bir_lowering=False, num_devices=1)
    aps = [nc.dram_tensor(k, a.shape, mybir.dt.from_np(a.dtype), kind="ExternalInput").ap() for k, a in arrays.items()]
    out = nc.dram_tensor("out_dram", (B, C, HW), mybir.dt.float32, kind="ExternalOutput").ap()
    aps[0] = aps[0].rearrange("(q b) c n -> b q c n", b=HALVES)
    hybrid_kernel(nc, *aps, out.rearrange("(q b) c n -> b q c n", b=HALVES))
    r = run_bass_kernel_spmd(nc, [arrays], core_ids=[0])
    return r.results[0]["out_dram"].reshape(B, C, SIDE, SIDE)
```
